# Optimizing a Trainium2 kernel written in Bass

```python
import numpy as np
import jax
import jax.numpy as jnp

def _softmax(x, axis=-1):
    return jax.nn.softmax(x, axis=axis)

def _gelu(x):
    return jax.nn.gelu(x, approximate=True)

def _silu(x):
    return jax.nn.silu(x)

def _sigmoid(x):
    return jax.nn.sigmoid(x)

def _layernorm(x, axis=-1, eps=1e-05):
    m = jnp.mean(x, axis=axis, keepdims=True)
    v = jnp.var(x, axis=axis, keepdims=True)
    return (x - m) / jnp.sqrt(v + eps)

def _scatter_add(tgt, idx, src, axis=0):
    return tgt.at[idx].add(src)

def _segment_sum(src, seg, n):
    return jax.ops.segment_sum(src, seg, n)
kernel_name = 'mk_cond_seq_d2_seqx_r4_4b4fdf'

def setup_inputs(seed: int=0):
    np.random.seed(seed)
    _w = jnp.asarray

    def _rec_inputs():
        import jax
        import jax.numpy as jnp
        _rk = jax.random.key(seed)
        x = -0.0005207 + 1.001 * jax.random.normal(jax.random.fold_in(_rk, 1), (32, 256, 256), jnp.float32)
        _lenS = 256 - jax.random.randint(jax.random.fold_in(_rk, 7), (32,), 0, max(1, 256 // 4) + 1, jnp.int32)
        _lenS2 = 256 - jax.random.randint(jax.random.fold_in(_rk, 8), (32,), 0, max(1, 256 // 4) + 1, jnp.int32)
        itok_B_34_63 = jax.random.randint(jax.random.fold_in(_rk, 12), (32,), 34, 64, jnp.int32)
        fside_Bx16xSxS_0 = -1.47943e-05 + 1.00017 * jax.random.normal(jax.random.fold_in(_rk, 13), (32, 16, 256, 256), jnp.float32)
        condB_dt = jax.random.uniform(jax.random.fold_in(_rk, 14), (32,), jnp.float32, 0.0, 0.981965)
        _validS = jnp.arange(256)[None, :] < _lenS[:, None]
        _validS2 = jnp.arange(256)[None, :] < _lenS2[:, None]
        _causal = jnp.tril(jnp.ones((256, 256), dtype=bool))
        mask_Bx1xSxS_bk0 = jnp.logical_not(jnp.broadcast_to(_validS[:, None, None, :], (32, 1, 256, 256)))
        return (x, itok_B_34_63, fside_Bx16xSxS_0, condB_dt, mask_Bx1xSxS_bk0)
    x, itok_B_34_63, fside_Bx16xSxS_0, condB_dt, mask_Bx1xSxS_bk0 = _rec_inputs()

    def _L0_cond_setup():
        import jax, jax.numpy as jnp
        import numpy as np
        import math
        D_MODEL = 256
        N_HEAD = 16
        HEAD_DIM = D_MODEL // N_HEAD
        D_FF = 1024
        NUM_STEPS = 100.0
        RESCALE = 4000.0
        EPS = 1e-05

        def _sin_emb(t):
            half = D_MODEL // 2
            x = t.astype(jnp.float32) / NUM_STEPS * RESCALE
            freqs = jnp.exp(jnp.arange(half, dtype=jnp.float32) * (-math.log(10000.0) / (half - 1)))
            e = x[:, None] * freqs[None, :]
            return jnp.concatenate([jnp.sin(e), jnp.cos(e)], axis=-1)

        def _ln(x):
            m = jnp.mean(x, axis=-1, keepdims=True)
            v = jnp.var(x, axis=-1, keepdims=True)
            return (x - m) / jnp.sqrt(v + EPS)

        def _gelu2(x):
            return x * jax.nn.sigmoid(1.702 * x)
        key = jax.random.key(seed)
        ks = jax.random.split(key, 24)
        B, S, D, F = (4, 128, D_MODEL, D_FF)
        std = 0.02
        inp = {'src': jax.random.normal(ks[0], (B, S, D), dtype=jnp.float32), 'src_mask': jax.random.randint(ks[1], (B, 1, S, S), 0, 2).astype(bool), 'timestep': jax.random.randint(ks[2], (B,), 0, 100, dtype=jnp.int32), 'attention_bias': jax.random.normal(ks[3], (B, N_HEAD, S, S), dtype=jnp.float32), 'W_ada': jax.random.normal(ks[4], (D, 2 * D), dtype=jnp.float32) * std, 'b_ada': jnp.zeros((2 * D,), dtype=jnp.float32), 'Wq': jax.random.normal(ks[5], (D, D), dtype=jnp.float32) * std, 'bq': jnp.zeros((D,), dtype=jnp.float32), 'Wk': jax.random.normal(ks[6], (D, D), dtype=jnp.float32) * std, 'bk': jnp.zeros((D,), dtype=jnp.float32), 'Wv': jax.random.normal(ks[7], (D, D), dtype=jnp.float32) * std, 'bv': jnp.zeros((D,), dtype=jnp.float32), 'Wo': jax.random.normal(ks[8], (D, D), dtype=jnp.float32) * std, 'bo': jnp.zeros((D,), dtype=jnp.float32), 'W1': jax.random.normal(ks[9], (D, F), dtype=jnp.float32) * std, 'b1': jnp.zeros((F,), dtype=jnp.float32), 'W2': jax.random.normal(ks[10], (F, D), dtype=jnp.float32) * std, 'b2': jnp.zeros((D,), dtype=jnp.float32), 'g2': jnp.ones((D,), dtype=jnp.float32), 'beta2': jnp.zeros((D,), dtype=jnp.float32)}
        return inp
    _L0_cond_all = _L0_cond_setup()
    _L0_cond_in = {k: v for k, v in _L0_cond_all.items() if k in ('W_ada', 'b_ada', 'Wq', 'bq', 'Wk', 'bk', 'Wv', 'bv', 'Wo', 'bo', 'W1', 'b1', 'W2', 'b2', 'g2', 'beta2')}
    del _L0_cond_all

    def _L1_cond_setup():
        import jax, jax.numpy as jnp
        import numpy as np
        B, NX, NY = (16, 256, 256)

        def _grad(f, axis):
            fm = jnp.moveaxis(f, axis, -1)
            g = (jnp.roll(fm, -1, -1) - jnp.roll(fm, 1, -1)) * 0.5
            g0 = (-3.0 * fm[..., 0] + 4.0 * fm[..., 1] - fm[..., 2]) * 0.5
            gN = (3.0 * fm[..., -1] - 4.0 * fm[..., -2] + fm[..., -3]) * 0.5
            g = g.at[..., 0].set(g0).at[..., -1].set(gN)
            return jnp.moveaxis(g, -1, axis)

        def _grad2(f, axis):
            fm = jnp.moveaxis(f, axis, -1)
            g = jnp.roll(fm, -1, -1) - 2.0 * fm + jnp.roll(fm, 1, -1)
            g0 = 2.0 * fm[..., 0] - 5.0 * fm[..., 1] + 4.0 * fm[..., 2] - fm[..., 3]
            gN = 2.0 * fm[..., -1] - 5.0 * fm[..., -2] + 4.0 * fm[..., -3] - fm[..., -4]
            g = g.at[..., 0].set(g0).at[..., -1].set(gN)
            return jnp.moveaxis(g, -1, axis)
        key = jax.random.key(seed)
        k1, k2, k3, k4 = jax.random.split(key, 4)
        f = jax.random.uniform(k1, (B, NX, NY), dtype=jnp.float32)
        A_grid = jax.random.normal(k2, (2, NX, NY), dtype=jnp.float32)
        B_grid = jax.random.uniform(k3, (3, NX, NY), dtype=jnp.float32)
        dt = jax.random.uniform(k4, (B,), dtype=jnp.float32)
        return {'f': f, 'A_grid': A_grid, 'B_grid': B_grid, 'dt': dt}
    _L1_cond_all = _L1_cond_setup()
    _L1_cond_in = {k: v for k, v in _L1_cond_all.items() if k in ('A_grid', 'B_grid')}
    del _L1_cond_all
    return {'x': x, 'itok_B_34_63': itok_B_34_63, 'fside_Bx16xSxS_0': fside_Bx16xSxS_0, 'condB_dt': condB_dt, 'mask_Bx1xSxS_bk0': mask_Bx1xSxS_bk0, 'L0_cond_W_ada': _L0_cond_in['W_ada'], 'L0_cond_b_ada': _L0_cond_in['b_ada'], 'L0_cond_Wq': _L0_cond_in['Wq'], 'L0_cond_bq': _L0_cond_in['bq'], 'L0_cond_Wk': _L0_cond_in['Wk'], 'L0_cond_bk': _L0_cond_in['bk'], 'L0_cond_Wv': _L0_cond_in['Wv'], 'L0_cond_bv': _L0_cond_in['bv'], 'L0_cond_Wo': _L0_cond_in['Wo'], 'L0_cond_bo': _L0_cond_in['bo'], 'L0_cond_W1': _L0_cond_in['W1'], 'L0_cond_b1': _L0_cond_in['b1'], 'L0_cond_W2': _L0_cond_in['W2'], 'L0_cond_b2': _L0_cond_in['b2'], 'L0_cond_g2': _L0_cond_in['g2'], 'L0_cond_beta2': _L0_cond_in['beta2'], 'L1_cond_A_grid': _L1_cond_in['A_grid'], 'L1_cond_B_grid': _L1_cond_in['B_grid']}

def reference(x, itok_B_34_63, fside_Bx16xSxS_0, condB_dt, mask_Bx1xSxS_bk0, L0_cond_W_ada, L0_cond_b_ada, L0_cond_Wq, L0_cond_bq, L0_cond_Wk, L0_cond_bk, L0_cond_Wv, L0_cond_bv, L0_cond_Wo, L0_cond_bo, L0_cond_W1, L0_cond_b1, L0_cond_W2, L0_cond_b2, L0_cond_g2, L0_cond_beta2, L1_cond_A_grid, L1_cond_B_grid):
    import jax
    import jax.numpy as jnp

    def _L0_cond_ref(src, src_mask, timestep, attention_bias, W_ada, b_ada, Wq, bq, Wk, bk, Wv, bv, Wo, bo, W1, b1, W2, b2, g2, beta2):
        import jax, jax.numpy as jnp
        import numpy as np
        import math
        D_MODEL = 256
        N_HEAD = 16
        HEAD_DIM = D_MODEL // N_HEAD
        D_FF = 1024
        NUM_STEPS = 100.0
        RESCALE = 4000.0
        EPS = 1e-05

        def _sin_emb(t):
            half = D_MODEL // 2
            x = t.astype(jnp.float32) / NUM_STEPS * RESCALE
            freqs = jnp.exp(jnp.arange(half, dtype=jnp.float32) * (-math.log(10000.0) / (half - 1)))
            e = x[:, None] * freqs[None, :]
            return jnp.concatenate([jnp.sin(e), jnp.cos(e)], axis=-1)

        def _ln(x):
            m = jnp.mean(x, axis=-1, keepdims=True)
            v = jnp.var(x, axis=-1, keepdims=True)
            return (x - m) / jnp.sqrt(v + EPS)

        def _gelu2(x):
            return x * jax.nn.sigmoid(1.702 * x)
        B, S, D = src.shape
        emb = jax.nn.silu(_sin_emb(timestep)) @ W_ada + b_ada
        scale, shift = jnp.split(emb[:, None, :], 2, axis=-1)
        x = _ln(src) * (1.0 + scale) + shift
        q = (x @ Wq + bq).reshape(B, S, N_HEAD, HEAD_DIM).transpose(0, 2, 1, 3)
        k = (x @ Wk + bk).reshape(B, S, N_HEAD, HEAD_DIM).transpose(0, 2, 1, 3)
        v = (x @ Wv + bv).reshape(B, S, N_HEAD, HEAD_DIM).transpose(0, 2, 1, 3)
        scores = jnp.einsum('bhqd,bhkd->bhqk', q / math.sqrt(HEAD_DIM), k)
        scores = scores + attention_bias
        scores = jnp.where(src_mask, -jnp.inf, scores.astype(jnp.float32))
        probs = jax.nn.softmax(scores, axis=-1).astype(v.dtype)
        ctx = jnp.einsum('bhqk,bhkd->bhqd', probs, v)
        ctx = ctx.transpose(0, 2, 1, 3).reshape(B, S, D)
        x = x + (ctx @ Wo + bo)
        h = _ln(x) * g2 + beta2
        ff = _gelu2(h @ W1 + b1) @ W2 + b2
        return x + ff

    def _L1_cond_ref(f, A_grid, B_grid, dt):
        import jax, jax.numpy as jnp
        import numpy as np
        B, NX, NY = (16, 256, 256)

        def _grad(f, axis):
            fm = jnp.moveaxis(f, axis, -1)
            g = (jnp.roll(fm, -1, -1) - jnp.roll(fm, 1, -1)) * 0.5
            g0 = (-3.0 * fm[..., 0] + 4.0 * fm[..., 1] - fm[..., 2]) * 0.5
            gN = (3.0 * fm[..., -1] - 4.0 * fm[..., -2] + fm[..., -3]) * 0.5
            g = g.at[..., 0].set(g0).at[..., -1].set(gN)
            return jnp.moveaxis(g, -1, axis)

        def _grad2(f, axis):
            fm = jnp.moveaxis(f, axis, -1)
            g = jnp.roll(fm, -1, -1) - 2.0 * fm + jnp.roll(fm, 1, -1)
            g0 = 2.0 * fm[..., 0] - 5.0 * fm[..., 1] + 4.0 * fm[..., 2] - fm[..., 3]
            gN = 2.0 * fm[..., -1] - 5.0 * fm[..., -2] + 4.0 * fm[..., -3] - fm[..., -4]
            g = g.at[..., 0].set(g0).at[..., -1].set(gN)
            return jnp.moveaxis(g, -1, axis)
        Af = A_grid[None] * f[:, None]
        Bf = B_grid[None] * f[:, None]
        gradv_Af = _grad(Af[:, 0], 1) + _grad(Af[:, 1], 2)
        gradvv_Bf = _grad2(Bf[:, 0], 1) + _grad2(Bf[:, 1], 2) + _grad(_grad(Bf[:, 2], 2), 1) + _grad(_grad(Bf[:, 2], 1), 2)
        df = -gradv_Af + gradvv_Bf * 0.5
        f_new = f + df * dt[:, None, None]
        return jnp.maximum(f_new, 0.0)
    x = _L0_cond_ref(x, mask_Bx1xSxS_bk0, itok_B_34_63, fside_Bx16xSxS_0, L0_cond_W_ada, L0_cond_b_ada, L0_cond_Wq, L0_cond_bq, L0_cond_Wk, L0_cond_bk, L0_cond_Wv, L0_cond_bv, L0_cond_Wo, L0_cond_bo, L0_cond_W1, L0_cond_b1, L0_cond_W2, L0_cond_b2, L0_cond_g2, L0_cond_beta2)
    x = _L1_cond_ref(x, L1_cond_A_grid, L1_cond_B_grid, condB_dt)
    return x

_drawn_inputs = setup_inputs


def setup_inputs(seed=0):
    import zlib

    import numpy as np

    out = dict(_drawn_inputs(seed))
    spreads = {'L0_cond_b_ada': (0.0, 0.1),
     'L0_cond_bq': (0.0, 0.8),
     'L0_cond_bk': (0.0, 0.8),
     'L0_cond_bv': (0.0, 0.1),
     'L0_cond_bo': (0.0, 0.1),
     'L0_cond_b1': (0.0, 0.1),
     'L0_cond_b2': (0.0, 0.1),
     'L0_cond_g2': (1.0, 0.6),
     'L0_cond_beta2': (0.0, 0.776)}
    factors = {'fside_Bx16xSxS_0': 6.8, 'L0_cond_Wq': 8.0, 'L0_cond_Wk': 8.0, 'L0_cond_Wv': 2.755}
    for name, (base, spread) in spreads.items():
        noise = np.random.default_rng([zlib.crc32(name.encode()), seed]).standard_normal(out[name].shape)
        drawn = base * np.exp(spread * noise) if base else spread * noise
        out[name] = jnp.asarray(drawn.astype(out[name].dtype))
    for name, factor in factors.items():
        out[name] = (out[name] * factor).astype(out[name].dtype)
    return out
```

```python
import concourse.bass as bass
from concourse import mybir
from contextlib import ExitStack

ALU = mybir.AluOpType
ACT = mybir.ActivationFunctionType
AXES = mybir.AxisListType
F32 = mybir.dt.float32
F32R = mybir.dt.float32r
I32 = mybir.dt.int32
U8 = mybir.dt.uint8

B, S, D, H, HD, FF = 32, 256, 256, 16, 16, 1024
P = 128
NT = S // P
NC = D // P
NF = FF // P
GROUP = 4
NG = H // GROUP
ROWS = 64
PARTS = 3
P_RING, PT_RING = 4, 8
LEAD = 3
EPS = 1e-5
NEG = -3.0e38
HUGE = 3.4e38
GELU = 1.702


def head_of(n):
    c, e, j = n // 8, (n // 4) % 2, n % 4
    return 8 * c + 2 * j + e


def build(nc, x, itok, fside, dt, mask, W_ada, b_ada, Wq, bq, Wk, bk, Wv, bv, Wo, bo, W1, b1, W2, b2,
          g2, beta2, A_grid, B_grid, freqs, stencils, out):
    ctx = ExitStack()
    with ctx:
        def sb(name, shape, dtype=F32):
            return ctx.enter_context(nc.sbuf_tensor(name, shape, dtype))

        def sem(name):
            return ctx.enter_context(nc.semaphore(name))

        ident = sb("ident", [P, P])
        ident_r = sb("ident_r", [P, P], F32R)
        wq_hl = sb("wq_hl", [P, 2, NC, D], F32R)
        wk_hl = sb("wk_hl", [P, 2, NC, D], F32R)
        wv_hl = sb("wv_hl", [P, 2, NC, D], F32R)
        wo_hl = sb("wo_hl", [P, 2, NC, D], F32R)
        w1_hl = sb("w1_hl", [P, 2, NC, FF], F32R)
        w2 = sb("w2", [P, NF, D])
        sten_w = sb("sten_w", [P, 2, NT, S])
        bqk = sb("bqk", [P, NC, 2])
        b1c = sb("b1c", [P, NF])
        b1s = sb("b1s", [P, NF])
        g2c = sb("g2c", [P, NC])
        be2c = sb("be2c", [P, NC])
        bv_row = sb("bv_row", [P, D])
        bo_row = sb("bo_row", [P, D])
        b2_row = sb("b2_row", [P, D])
        half = sb("half", [P, NT])
        emb = sb("emb", [P, 4, B])
        dt_row = sb("dt_row", [P, B])
        grids = sb("grids", [P, 6, NT, D])
        gA0, gB0, gR, gL, gC, gB2 = (grids[:, k] for k in range(6))
        edge = sb("edge", [P, NT, 4, 4])

        bias = sb("bias", [P, NG, GROUP, NT, S])
        mask_w = sb("mask_w", [P, NT, S // 4], I32)
        mneg = sb("mneg", [P, NT, S])
        src = sb("src", [P, NT, D])
        xn = sb("xn", [P, NT, D])
        xTf = sb("xTf", [P, NC, S])
        xT = sb("xT", [P, 2, 2, NC, S], F32R)
        cur = sb("cur", [P, 2, 4])
        dcur = sb("dcur", [P, 1])
        bad = sb("bad", [P, 4])
        qkf = xTf
        qk = sb("qk", [P, 2, 2, S], F32R)
        Qs = sb("Qs", [P, H // 2, S], F32R)
        Ks = sb("Ks", [P, H, S], F32R)
        V = sb("V", [P, NT, H, 32])
        nmax = sb("nmax", [P, H, NT])
        Pb = sb("Pb", [P, P_RING, NT, S])
        PT = sb("PT", [P, PT_RING, NT, S])
        sums = sb("sums", [P, 2, NT, H])
        rec = sb("rec", [P, NT, H])
        rbc = sb("rbc", [P, NT, H, HD])
        cT = sb("cT", [P, 2, NC, S], F32R)
        stat1 = sb("stat1", [P, NT, 6])
        mv1 = sb("mv1", [P, NT, 2])
        ve1 = sb("ve1", [P, NT])
        rs1 = sb("rs1", [P, NT])
        stat2 = sb("stat2", [P, NT, 6])
        mv2 = sb("mv2", [P, NT, 2])
        ve2 = sb("ve2", [P, NT])
        rs2 = sb("rs2", [P, NT])
        x2 = sb("x2", [P, NT, D])
        cn = x2
        x2b = sb("x2b", [P, NT, D])
        hn = xn
        hTf = sb("hTf", [P, NC, S])
        rTs = hTf
        hT = sb("hT", [P, 2, NC, S], F32R)
        th = sb("th", [P, 2, 2, S])
        g = sb("g", [P, NF, S])
        x3 = sb("x3", [P, NT, D])
        pR = sb("pR", [P, NT, D])
        pL = sb("pL", [P, NT, D])
        pC = pR
        tt = sb("tt", [P, NT, D])
        b2f = x2b
        a0f = sb("a0f", [P, NT, D])
        u1 = a0f
        u1e = sb("u1e", [P, NT, 2])
        u2 = sb("u2", [P, NT, D])
        ed = sb("ed", [P, NT, 4, 4])
        yy = tt
        zf = pL

        def bank(name, shape):
            return ctx.enter_context(nc.psum_tensor(name, shape, F32))

        pS = [bank(f"pS{k}", [P, NT, S]) for k in range(2)]
        pT = [bank(f"pT{k}", [P, NT, S]) for k in range(2)]
        pC_ = bank("pCtx", [P, NC, S])
        M0 = bank("M0", [P, 2, S])
        M1 = bank("M1", [P, 2, S])
        M2 = bank("M2", [P, NT, D])

        ld_w = [sem(f"ld_w{k}") for k in range(6)]
        ld_c = sem("ld_c")
        ld_g = sem("ld_g")
        ld_w2 = sem("ld_W2")
        ld_src = sem("ld_src")
        ld_mask = sem("ld_mask")
        ld_bias = [sem(f"ld_bias{k}") for k in range(NG)]
        scat = [sem(f"scat{c}") for c in range(NC)]
        stored = sem("stored")
        s_id = sem("s_id")
        s_cst = sem("s_cst")
        s_emb = sem("s_emb")
        s_sin = sem("s_sin")
        s_embmm = sem("s_embmm")
        s_tanh0 = sem("s_tanh0")
        s_split = sem("s_split")
        s_stat1 = sem("s_stat1"); s_mv1 = sem("s_mv1"); s_ve1 = sem("s_ve1"); s_rs1 = sem("s_rs1")
        s_stat2 = sem("s_stat2"); s_mv2 = sem("s_mv2"); s_ve2 = sem("s_ve2"); s_rs2 = sem("s_rs2")
        s_cur = sem("s_cur"); s_dcur = sem("s_dcur"); s_lnk = sem("s_lnk")
        s_xn = sem("s_xn"); s_xT = sem("s_xT"); s_xTf = sem("s_xTf"); s_xhi = sem("s_xhi"); s_xhl = sem("s_xhl")
        s_qk = sem("s_qk"); s_qkf = sem("s_qkf"); s_qhi = sem("s_qhi"); s_qhl = sem("s_qhl")
        s_zero = sem("s_zero")
        s_v = sem("s_v"); s_vev = sem("s_vev")
        s_mneg = sem("s_mneg"); s_madd = sem("s_madd")
        s_S = sem("s_S"); s_ttr = sem("s_ttr"); s_exp = sem("s_exp")
        s_T = sem("s_T"); s_ptA = sem("s_ptA"); s_ptD = sem("s_ptD"); s_ctx = sem("s_ctx")
        s_rec = sem("s_rec"); s_rbc = sem("s_rbc"); s_rT = sem("s_rT"); s_rTs = sem("s_rTs")
        s_cn = sem("s_cn"); s_chi = sem("s_chi"); s_chl = sem("s_chl")
        s_wo = sem("s_wo"); s_x2 = sem("s_x2"); s_x2b = sem("s_x2b"); s_hn = sem("s_hn")
        s_hT = sem("s_hT"); s_hTf = sem("s_hTf"); s_hhi = sem("s_hhi"); s_hhl = sem("s_hhl")
        s_f1 = sem("s_f1"); s_tanh = sem("s_tanh"); s_z = sem("s_z"); s_g = sem("s_g")
        s_f2 = sem("s_f2"); s_x3 = sem("s_x3")
        s_b2f = sem("s_b2f"); s_a0f = sem("s_a0f"); s_u2 = sem("s_u2")
        s_pRL = sem("s_pRL"); s_tt = sem("s_tt"); s_pC = sem("s_pC"); s_ed = sem("s_ed")
        s_d1 = sem("s_d1"); s_u1 = sem("s_u1")
        s_st = sem("s_st"); s_y = sem("s_y"); s_zf = sem("s_zf"); s_relu = sem("s_relu")

        FULL = dict(att=True, nxt=True, post=True, sten=True)

        def run(eng, prologue, body):
            prologue()
            body(0, 0, att=True, nxt=True, post=False, sten=False)
            body(0, 1, att=True, nxt=True, post=True, sten=False)
            with eng.Fori(1, B // 2 - 1) as j:
                body(j, 0, **FULL)
                body(j, 1, **FULL)
            body(B // 2 - 1, 0, **FULL)
            body(B // 2 - 1, 1, att=True, nxt=False, post=True, sten=True)
            body(B // 2, 0, att=False, nxt=False, post=True, sten=True)
            body(B // 2, 1, att=False, nxt=False, post=False, sten=True)

        def by_itself(eng, *waits):
            for _, v in waits:
                eng.compute_val(v)
            eng.wait_ge(s_id, 3)
            for s_, v in waits:
                eng.wait_ge(s_, v)

        block = ctx.enter_context(nc.Block())

        @block.sync
        def _(sp):
            def tok(ap):
                return ap.rearrange("(t p) n -> p t n", p=P)

            def at(ap, i):
                return ap[i] if isinstance(i, int) else ap[bass.ds(i, 1)].rearrange("o a n -> (o a) n")

            def load_src(i):
                sp.dma_start(src[:], tok(at(x, i))).then_inc(ld_src, 16)

            def load_mask(i):
                sp.dma_start(mask_w[:], tok(at(mask, i))).then_inc(ld_mask, 16)

            def load_bias(i, n):
                c, e = n // 2, n % 2
                for t in range(NT):
                    rows = (fside[i] if isinstance(i, int) else
                            fside[bass.ds(i, 1)].rearrange("o h q k -> (o h) q k"))
                    part = rows[8 * c + e:8 * c + 8:2, t * P:(t + 1) * P, :].rearrange("h p k -> p h k")
                    sp.dma_start(bias[:, n, :, t, :], part).then_inc(ld_bias[n], 16)

            def scatter(c):
                for s in range(2):
                    for r in range(PARTS):
                        for w, high_low in ((0, (0, 1, 0)), (1, (0, 0, 1))):
                            rows = slice(ROWS * s + HD * r, ROWS * s + HD * (r + 1))
                            into = Qs[rows, 4 * c:4 * c + 4, :] if w == 0 else Ks[rows, 8 * c + s:8 * c + 8:2, :]
                            sp.dma_start(into.bitcast(F32), qk[64 * s:64 * s + 64, high_low[r], w, :].bitcast(F32))\
                              .then_inc(scat[c], 16)

            def prologue():
                load_src(0)
                small = [(b_ada.rearrange("(m p) -> p m", p=P), emb[:, 0, 0:4]),
                         (freqs.rearrange("(p o) -> p o", o=1), emb[:, 0, 4:5]),
                         (bq.rearrange("(c p) -> p c", p=P), bqk[:, :, 0]),
                         (bk.rearrange("(c p) -> p c", p=P), bqk[:, :, 1]),
                         (b1.rearrange("(m p) -> p m", p=P), b1c[:]),
                         (g2.rearrange("(c p) -> p c", p=P), g2c[:]),
                         (beta2.rearrange("(c p) -> p c", p=P), be2c[:])]
                with nc.allow_non_contiguous_dma(reason="small vectors, once"):
                    for from_, into in small:
                        sp.dma_start(into, from_).then_inc(ld_c, 16)
                for from_, into in ((bv, bv_row), (bo, bo_row), (b2, b2_row), (dt, dt_row)):
                    sp.dma_start(into[:], from_.partition_broadcast(P)).then_inc(ld_c, 16)
                sp.dma_start(rbc[:, 0, 0:2, :].rearrange("p a b -> p (a b)").bitcast(I32),
                             itok.partition_broadcast(P)).then_inc(ld_c, 16)
                ring = PT[:].rearrange("p a t s -> p (a t s)")
                sp.dma_start(g[:, 0:4, :].rearrange("p a b -> p (a b)").rearrange("p (k n) -> p k n", k=2),
                             W_ada.rearrange("(k p) n -> p k n", p=P)).then_inc(ld_w[5], 16)
                for k, w in enumerate((Wq, Wk, Wv, Wo)):
                    sp.dma_start(ring[:, k * NC * D:(k + 1) * NC * D].rearrange("p (k n) -> p k n", k=NC),
                                 w.rearrange("(k p) n -> p k n", p=P)).then_inc(ld_w[k], 16)
                load_mask(0)
                load_bias(0, 0)
                sp.dma_start(ring[:, 2048:4096].rearrange("p (k n) -> p k n", k=NC),
                             W1.rearrange("(k p) n -> p k n", p=P)).then_inc(ld_w[4], 16)
                for n in range(1, NG):
                    load_bias(0, n)
                sp.dma_start(w2[:], W2.rearrange("(k p) n -> p k n", p=P)).then_inc(ld_w2, 16)
                for g_, into in ((A_grid[0], gA0), (B_grid[0], gB0), (A_grid[1], gR), (B_grid[1], gC), (B_grid[2], gB2)):
                    sp.dma_start(into, tok(g_)).then_inc(ld_g, 16)
                sp.dma_start(sten_w[:], stencils.rearrange("m (k p) n -> p m k n", p=P)).then_inc(ld_g, 16)
                for c in range(NC):
                    if c == 0:
                        sp.wait_ge(s_zero, 2)
                    sp.wait_ge(s_qhl, c + 1)
                    scatter(c)

            def body(j, par, att, nxt, post, sten):
                i = j * 2 + par
                if nxt:
                    by_itself(sp, (s_xn, (i + 1) * 2))
                    load_src(i + 1)
                    by_itself(sp, (s_mneg, i + 1))
                    load_mask(i + 1)
                    by_itself(sp, (s_exp, i * 32 + 8))
                    load_bias(i + 1, 0)
                if sten:
                    by_itself(sp, (s_relu, i - 1))
                    sp.dma_start(tok(at(out, i - 2)), zf[:]).then_inc(stored, 16)
                if nxt:
                    by_itself(sp, (s_exp, i * 32 + 16))
                    load_bias(i + 1, 1)
                    by_itself(sp, (s_qhl, (i + 2) * 2 - 1), (s_S, i * H + 8))
                    scatter(0)
                    by_itself(sp, (s_exp, i * 32 + 24))
                    load_bias(i + 1, 2)
                    by_itself(sp, (s_qhl, (i + 2) * 2), (s_S, i * H + 16))
                    scatter(1)
                    by_itself(sp, (s_exp, i * 32 + 32))
                    load_bias(i + 1, 3)

            run(sp, prologue, body)
            sp.wait_ge(stored, 16 * B)

        @block.gpsimd
        def _(pool):
            def mask_bias(i, n):
                if n == 0:
                    if isinstance(i, int) and i == 0:
                        pool.wait_ge(ld_mask, 16)
                    else:
                        by_itself(pool, (ld_mask, i * 16 + 16), (s_madd, i * H))
                    pool.tensor_scalar(mneg[:], mask_w[:].bitcast(U8), NEG, 1.0, ALU.mult, ALU.mult).then_inc(s_mneg, 1)
                    pool.wait_ge(s_mneg, i + 1)
                if n % GROUP == 0:
                    pool.wait_ge(ld_bias[n // GROUP], i * 32 + 32)
                b = bias[:, n // GROUP, n % GROUP]
                pool.tensor_tensor(b, b, mneg[:], ALU.add).then_inc(s_madd, 1)

            def power(mv, ve, rs, s_mv, s_ve, s_rs, i):
                by_itself(pool, (s_mv, (i + 1) * 2))
                pool.tensor_scalar(ve[:], mv[:, :, 1], EPS, 1.0, ALU.add, ALU.mult).then_inc(s_ve, 1)
                pool.wait_ge(s_ve, i + 1)
                pool.tensor_tensor(rs[:], ve[:], half[:], ALU.pow).then_inc(s_rs, 1)

            def prologue():
                pool.memset(ident[:], 0.0).then_inc(s_id, 1)
                pool.memset(half[:], -0.5).then_inc(s_id, 1)
                pool.wait_ge(s_id, 2)
                pool.affine_select(out=ident[:], in_=ident[:], compare_op=ALU.not_equal, fill=1.0, base=0,
                                   pattern=[[-1, P]], channel_multiplier=1).then_inc(s_id, 1)
                power(mv1, ve1, rs1, s_mv1, s_ve1, s_rs1, 0)
                pool.memset(Ks[:].bitcast(F32), 0.0).then_inc(s_zero, 1)
                pool.memset(Qs[:].bitcast(F32), 0.0).then_inc(s_zero, 1)
                pool.memset(V[:], 0.0).then_inc(s_zero, 1)
                for n in range(LEAD):
                    mask_bias(0, n)

            def body(j, par, att, nxt, post, sten):
                i = j * 2 + par
                b = i - 1
                first = isinstance(b, int) and b == 0
                for n in range(H):
                    if sten:
                        d = i - 2
                        if n == 0:
                            pool.wait_ge(s_x3, d + 1)
                            if not (isinstance(d, int) and d == 0):
                                pool.wait_ge(s_st, d)
                            pool.tensor_tensor(b2f[:], x3[:], gB2, ALU.mult).then_inc(s_b2f, 1)
                            pool.tensor_tensor(a0f[:], x3[:], gA0, ALU.mult).then_inc(s_a0f, 1)
                        if n == 1:
                            pool.tensor_tensor(u2[:], x3[:], gB0, ALU.mult).then_inc(s_u2, 1)
                    if post and n == 2:
                        if first:
                            pool.wait_ge(s_rec, 1)
                        else:
                            by_itself(pool, (s_rec, i), (s_rT, b))
                        pool.tensor_copy(rbc[:].rearrange("p t h d -> p (t h) d"),
                                         rec[:].rearrange("p t (h o) -> p (t h) o", o=1).to_broadcast([P, NT * H, HD]))\
                            .then_inc(s_rbc, 1)
                    if nxt and n == 3:
                        power(mv1, ve1, rs1, s_mv1, s_ve1, s_rs1, i + 1)
                    if post and n == 6:
                        power(mv2, ve2, rs2, s_mv2, s_ve2, s_rs2, b)
                    if post and n == 7:
                        if not (isinstance(b, int) and b == 0):
                            pool.wait_ge(s_x3, b)
                            pool.wait_ge(s_u1, b * 2)
                        for t in range(NT):
                            pool.tensor_tensor(x2b[:, t], x2[:, t], b2_row[:], ALU.add).then_inc(s_x2b, 1)
                    if n + LEAD < H:
                        if att:
                            mask_bias(i, n + LEAD)
                    elif nxt:
                        mask_bias(i + 1, n + LEAD - H)

            run(pool, prologue, body)

        @block.tensor
        def _(pe):
            mm = nc.tensor.matmul

            def split_mm(into, lhs, rhs, k, nk, close=True):
                for m, (a, b) in enumerate(((0, 0), (1, 0), (0, 1))):
                    last = mm(into, lhs[a], rhs[b], start=(k == 0 and m == 0),
                              stop=(close and k == nk - 1 and m == 2))
                return last

            def transposes(into, from_):
                for c in range(2):
                    for t in range(2):
                        last = nc.tensor.transpose(into[:, c, t * P:(t + 1) * P], from_(t, c), ident[:])
                return last

            def x_transposed(i):
                pe.wait_ge(s_xn, (i + 1) * 2)
                transposes(M1, lambda t, c: xn[:, t, c * P:(c + 1) * P]).then_inc(s_xT, 1)

            def qk_product(i, par, c, M):
                for w, wt in ((0, wq_hl), (1, wk_hl)):
                    for k in range(NC):
                        last = split_mm(M[:, w, :], [wt[:, a, k, c * P:(c + 1) * P] for a in (0, 1)],
                                        [xT[:, par, a, k, :] for a in (0, 1)], k, NC)
                last.then_inc(s_qk, 1)

            def transposed_probs(i, n):
                pe.wait_ge(s_exp, i * 32 + 2 * n + 2)
                if n >= 2 or not (isinstance(i, int) and i == 0):
                    pe.wait_ge(s_ptD if n % 2 else s_ptA, i * 8 + n // 2)
                for k in range(NT):
                    for t in range(NT):
                        last = nc.tensor.transpose(pT[n % 2][:, k, t * P:(t + 1) * P],
                                                   Pb[:, n % P_RING, t, k * P:(k + 1) * P], ident[:])
                last.then_inc(s_T, 1)

            def context(i, par, gr):
                pe.wait_ge(s_ptA, i * 8 + 2 * gr + 2)
                pe.wait_ge(s_ptD, i * 8 + 2 * gr + 2)
                if gr == 0:
                    pe.wait_ge(s_vev, i + 1)
                    if not (isinstance(i, int) and i == 0):
                        pe.wait_ge(s_cn, i)
                c, e = gr // 2, gr % 2
                for k in range(NT):
                    for q in range(GROUP):
                        n = gr * GROUP + q
                        last = mm(pC_[32 * q:32 * q + 32, c, :], V[:, k, head_of(n), :],
                                  PT[:, n % PT_RING, k, :], start=(e == 0 and k == 0),
                                  stop=(e == 1 and k == NT - 1))
                last.then_inc(s_ctx, 1)

            def prologue():
                pe.wait_ge(s_emb, 1)
                pe.wait_ge(ld_w[5], 16)
                wa = g[:, 0:4, :].rearrange("p a b -> p (a b)").rearrange("p (k n) -> p k n", k=2)
                silu = g[:, 4, 64:128].rearrange("p (k b) -> p k b", k=2)
                for m in range(4):
                    for k in range(2):
                        last = mm(M2[:, 0, m * B:(m + 1) * B], wa[:, k, m * P:(m + 1) * P], silu[:, k, :],
                                  start=(k == 0), stop=(k == 1))
                last.then_inc(s_embmm, 1)
                pe.wait_ge(s_id, 3)
                x_transposed(0)
                pe.wait_ge(s_split, 2)
                pe.wait_ge(s_xhl, 1)
                qk_product(0, 0, 0, M1)
                qk_product(0, 0, 1, M0)

            def body(j, par, att, nxt, post, sten):
                i = j * 2 + par
                b = i - 1
                zero = isinstance(i, int) and i == 0
                first = isinstance(b, int) and b == 0
                for n in range(H):
                    if att:
                        if n % 8 == 0:
                            pe.wait_ge(scat[n // 8], (i + 1) * (16 * 4 * PARTS))
                        if n >= 2 or not zero:
                            pe.wait_ge(s_ttr, i * 32 + 2 * n - 2)
                        h = head_of(n)
                        for t in range(NT):
                            last = mm(pS[n % 2][:, t, :], Qs[:, h // 2, t * P:(t + 1) * P], Ks[:, h, :],
                                      start=True, stop=True)
                        last.then_inc(s_S, 1)
                    if att and n == 0:
                        if zero:
                            pe.wait_ge(s_split, 4)
                        pe.wait_ge(s_qkf, (i + 1) * 4)
                        for t in range(NT):
                            for k in range(NC):
                                last = split_mm(M0[:, t, :], [xT[:, par, a, k, t * P:(t + 1) * P] for a in (0, 1)],
                                                [wv_hl[:, a, k, :] for a in (0, 1)], k, NC)
                        last.then_inc(s_v, 1)
                    if post and n == 2:
                        if not first:
                            pe.wait_ge(s_tanh, b * 8)
                            pe.wait_ge(s_z, b * 8)
                        pe.wait_ge(s_rbc, i)
                        transposes(M1, lambda t, c: rbc[:, t, 8 * c:8 * c + 8, :].rearrange("p h d -> p (h d)"))\
                            .then_inc(s_rT, 1)
                    if sten and n == 3:
                        pe.wait_ge(s_u1, (i - 1) * 2)
                        pe.wait_ge(s_u2, i - 1)
                        pe.wait_ge(s_x3, i - 1)
                        for t in range(NT):
                            for m, u in enumerate((u1, u2)):
                                for k in range(NT):
                                    last = mm(M2[:, t, :], sten_w[:, m, k, t * P:(t + 1) * P], u[:, k, :],
                                              start=(m == 0 and k == 0), stop=(m == 1 and k == NT - 1))
                        last.then_inc(s_st, 1)
                    if post and n == 4:
                        if att:
                            pe.wait_ge(s_vev, i + 1)
                        pe.wait_ge(s_chl, i)
                        for t in range(NT):
                            for k in range(NC):
                                split_mm(M0[:, t, :], [cT[:, a, k, t * P:(t + 1) * P] for a in (0, 1)],
                                         [wo_hl[:, a, k, :] for a in (0, 1)], k, NC, close=False)
                            for c in range(NC):
                                for a in (0, 1):
                                    last = mm(M0[:, t, c * P:(c + 1) * P], xT[:, 1 - par, a, c, t * P:(t + 1) * P],
                                              ident_r[:], start=False, stop=(c == NC - 1 and a == 1))
                        last.then_inc(s_wo, 1)
                    if nxt and n == 5:
                        if post:
                            pe.wait_ge(s_rTs, i)
                        x_transposed(i + 1)
                    if post and n == 6:
                        pe.wait_ge(s_hn, i * 2)
                        transposes(M0, lambda t, c: hn[:, t, c * P:(c + 1) * P]).then_inc(s_hT, 1)
                    if nxt and n == 7:
                        pe.wait_ge(s_xhl, i + 2)
                        qk_product(i + 1, 1 - par, 0, M1)
                    if post and 8 <= n < 12:
                        f = n - 8
                        M = (M0, M1)[f % 2]
                        if f == 0:
                            pe.wait_ge(s_hhl, i)
                        if f == 1 and nxt:
                            pe.wait_ge(s_qkf, (i + 1) * 4 + 2)
                        if f >= 2:
                            pe.wait_ge(s_tanh, b * 8 + 2 * f - 2)
                            pe.wait_ge(s_z, b * 8 + 2 * f - 2)
                        for m in range(2):
                            for k in range(NC):
                                last = split_mm(M[:, m, :],
                                                [w1_hl[:, a, k, (2 * f + m) * P:(2 * f + m + 1) * P] for a in (0, 1)],
                                                [hT[:, a, k, :] for a in (0, 1)], k, NC)
                        last.then_inc(s_f1, 1)
                    if nxt and n == 12:
                        if post:
                            pe.wait_ge(s_tanh, b * 8 + 6)
                            pe.wait_ge(s_z, b * 8 + 6)
                        qk_product(i + 1, 1 - par, 1, M0)
                    if post and 11 <= n < 15:
                        t, part = (n - 11) // 2, (n - 11) % 2
                        if n == 11 and sten:
                            pe.wait_ge(s_y, i - 1)
                        if n == 11 and first:
                            pe.wait_ge(ld_w2, 16)
                        pe.wait_ge(s_g, b * 4 + 2 * part + 2)
                        for f in range(4 * part, 4 * part + 4):
                            last = mm(M2[:, t, :], g[:, f, t * P:(t + 1) * P], w2[:, f, :],
                                      start=(f == 0), stop=(f == NF - 1))
                        if n == 14:
                            last.then_inc(s_f2, 1)
                    if n >= 2 and att:
                        transposed_probs(i, n - 2)
                    if n < 2 and post:
                        transposed_probs(b, n - 2 + H)
                    if n % GROUP == 2:
                        gr = n // GROUP - 1
                        if gr >= 0 and att:
                            context(i, par, gr)
                        if gr < 0 and post:
                            context(b, 1 - par, NG - 1)

            run(pe, prologue, body)

        @block.scalar
        def _(act):
            ident_f = ACT.Identity

            def x_evac(i, par):
                act.wait_ge(s_xT, i + 1)
                act.wait_ge(s_cur, i + 1)
                for c in range(NC):
                    if not (isinstance(i, int) and i == 0) and c == 0:
                        act.wait_ge(s_qhl, i * 2)
                    act.activation(xTf[:, c], M1[:, c], ident_f, bias=cur[:, par, 2 + c:3 + c],
                                   scale=cur[:, par, c:c + 1]).then_inc(s_xTf, 1)

            def qk_evac(i, c, M):
                act.wait_ge(s_qk, i * 2 + c + 1)
                if c > 0:
                    act.wait_ge(s_qhl, i * 2 + c)
                else:
                    act.wait_ge(s_xhl, i + 1)
                act.activation(qkf[:, 0], M[:, 0], ident_f, bias=bqk[:, c, 0:1], scale=HD ** -0.5).then_inc(s_qkf, 1)
                act.activation(qkf[:, 1], M[:, 1], ident_f, bias=bqk[:, c, 1:2]).then_inc(s_qkf, 1)

            def probs_evac(i, n):
                act.wait_ge(s_T, i * H + n + 1)
                if not (isinstance(i, int) and i == 0 and n < PT_RING):
                    act.wait_ge(s_ctx, i * NG + n // GROUP - 1)
                act.activation(PT[:, n % PT_RING], pT[n % 2][:], ACT.Copy).then_inc(s_ptA, 1)

            def prologue():
                act.wait_ge(s_cst, 1)
                ang = g[:, 4, 0:64]
                act.activation(g[:, 5, 0:64], ang, ACT.Sin).then_inc(s_sin, 1)
                act.wait_ge(s_sin, 1)
                act.activation(g[:, 5, 64:128], g[:, 5, 0:64], ACT.Tanh, scale=0.5).then_inc(s_tanh0, 1)
                x_evac(0, 0)
                qk_evac(0, 0, M1)
                qk_evac(0, 1, M0)

            def body(j, par, att, nxt, post, sten):
                i = j * 2 + par
                b = i - 1
                zero = isinstance(i, int) and i == 0
                first = isinstance(b, int) and b == 0
                for n in range(H):
                    if att:
                        for t in range(NT):
                            act.wait_ge(s_ttr, i * 32 + 2 * n + t + 1)
                            if t == 0 and (n >= P_RING or not zero):
                                act.wait_ge(s_T, i * H + n - P_RING + 1)
                            act.activation(Pb[:, n % P_RING, t], bias[:, n // GROUP, n % GROUP, t], ACT.Exp, scale=-1.0,
                                           bias=nmax[:, n, t:t + 1],
                                           accum_out=sums[:, par, t, head_of(n):head_of(n) + 1]).then_inc(s_exp, 1)
                    if n % 2 == 0:
                        if n >= 2 and att:
                            probs_evac(i, n - 2)
                        if n < 2 and post:
                            probs_evac(b, n - 2 + H)
                    if post and n == 2:
                        act.wait_ge(s_rT, i)
                        if not first:
                            act.wait_ge(s_hhl, b)
                        act.activation(rTs[:], M1[:], ACT.Copy).then_inc(s_rTs, 1)
                    if sten and n == 4:
                        act.wait_ge(s_zf, i - 1)
                        act.activation(zf[:], zf[:], ACT.Relu).then_inc(s_relu, 1)
                    if nxt and n == 5:
                        x_evac(i + 1, 1 - par)
                    if post and n == 6:
                        act.wait_ge(s_hT, i)
                        act.wait_ge(s_cn, i)
                        for c in range(NC):
                            act.activation(hTf[:, c], M0[:, c], ident_f, bias=be2c[:, c:c + 1],
                                           scale=g2c[:, c:c + 1]).then_inc(s_hTf, 1)
                    if nxt and n == 7:
                        qk_evac(i + 1, 0, M1)
                    if post and 8 <= n < 12:
                        f = n - 8
                        act.wait_ge(s_f1, b * 4 + f + 1)
                        if f >= 2 or not first:
                            act.wait_ge(s_g, b * 4 + f - 1)
                        for m in range(2):
                            act.activation(th[:, f % 2, m], (M0, M1)[f % 2][:, m], ACT.Tanh, scale=GELU / 2,
                                           bias=b1s[:, 2 * f + m:2 * f + m + 1]).then_inc(s_tanh, 1)
                    if nxt and n == 12:
                        qk_evac(i + 1, 1, M0)

            run(act, prologue, body)

        @block.vector
        def _(dve):
            steps = [0]

            def link(ins):
                steps[0] += 1
                ins.then_inc(s_lnk, 1)
                dve.wait_ge(s_lnk, steps[0])

            def column(i):
                return slice(i, i + 1) if isinstance(i, int) else bass.ds(i, 1)

            def norm(i, from_, stat, mv, s_stat, s_mv):
                for t in range(NT):
                    dve.bn_stats(stat[:, t], from_[:, t]).then_inc(s_stat, 1)
                by_itself(dve, (s_stat, (i + 1) * 2))
                for t in range(NT):
                    dve.bn_aggr(mv[:, t], stat[:, t]).then_inc(s_mv, 1)

            def apply_norm(into, from_, mv, rs, s_out):
                for t in range(NT):
                    dve.tensor_scalar(into[:, t], from_[:, t], mv[:, t, 0:1], rs[:, t:t + 1],
                                      ALU.subtract, ALU.mult).then_inc(s_out, 1)

            def norm1(i, par):
                dve.wait_ge(ld_src, (i + 1) * 16)
                norm(i, src, stat1, mv1, s_stat1, s_mv1)

            def cur_copy(i, par):
                dve.tensor_copy(cur[:, par].rearrange("p (a o) -> p a o", o=1), emb[:, :, column(i)]).then_inc(s_cur, 1)

            def apply1(i):
                dve.wait_ge(s_rs1, i + 1)
                if not (isinstance(i, int) and i == 0):
                    dve.wait_ge(s_xT, i)
                if not (isinstance(i, int) and i <= 2):
                    dve.wait_ge(s_hT, i - 2)
                apply_norm(xn, src, mv1, rs1, s_xn)

            def x_split(i, par):
                dve.wait_ge(s_xTf, (i + 1) * 2)
                dve.tensor_copy(xT[:, par, 0], xTf[:]).then_inc(s_xhi, 1)
                dve.wait_ge(s_xhi, i + 1)
                dve.tensor_tensor(xT[:, par, 1], xTf[:], xT[:, par, 0].bitcast(F32), ALU.subtract).then_inc(s_xhl, 1)

            def qk_split(i, c):
                dve.wait_ge(s_qkf, i * 4 + 2 * c + 2)
                if c == 1:
                    dve.wait_ge(scat[0], (i + 1) * (16 * 4 * PARTS))
                elif not (isinstance(i, int) and i == 0):
                    dve.wait_ge(scat[1], i * (16 * 4 * PARTS))
                dve.tensor_copy(qk[:, 0], qkf[:]).then_inc(s_qhi, 1)
                dve.wait_ge(s_qhi, i * 2 + c + 1)
                dve.tensor_tensor(qk[:, 1], qkf[:], qk[:, 0].bitcast(F32), ALU.subtract).then_inc(s_qhl, 1)

            def probs_evac(i, n):
                dve.wait_ge(s_T, i * H + n + 1)
                if not (isinstance(i, int) and i == 0 and n < PT_RING):
                    dve.wait_ge(s_ctx, i * NG + n // GROUP - 1)
                dve.tensor_copy(PT[:, n % PT_RING], pT[n % 2][:]).then_inc(s_ptD, 1)

            def prologue():
                dve.wait_ge(ld_c, 16 * 12)
                ti = rbc[:, 0, 0:2, :].rearrange("p a b -> p (a b)")
                tf, kk, tmp = g[:, 6, 0:32], g[:, 6, 64:96], g[:, 6, 96:128]
                ang = g[:, 4, 0:64].rearrange("p (k b) -> p k b", k=2)
                fr = emb[:, 0, 4:5]
                link(dve.tensor_copy(bad[:, 0:4], emb[:, 0, 0:4]))
                link(dve.tensor_copy(tf, ti.bitcast(I32)))
                link(dve.tensor_scalar(tf, tf, 0.01, 4000.0, ALU.mult, ALU.mult))
                link(dve.tensor_scalar(tf, tf, fr, None, ALU.mult))
                magic = 1.5 * 2 ** 23
                link(dve.tensor_scalar(kk, tf, 0.15915494309189535, magic, ALU.mult, ALU.add))
                link(dve.tensor_scalar(kk, kk, magic, None, ALU.subtract))
                two_pi = 6.283185307179586
                c1 = 6.28125
                c2 = round((two_pi - c1) * 2 ** 20) / 2 ** 20
                c3 = two_pi - c1 - c2
                for cc in (c1, c2, c3):
                    link(dve.scalar_tensor_tensor(out=tf, in0=kk, scalar=-cc, in1=tf, op0=ALU.mult, op1=ALU.add))
                pi = 3.1415925
                link(dve.tensor_scalar(ang[:, 0, :], tf, pi, -pi, ALU.min, ALU.max))
                link(dve.tensor_scalar(tf, tf, two_pi / 4, None, ALU.add))
                link(dve.tensor_scalar(tmp, tf, two_pi / 2, -two_pi, ALU.is_gt, ALU.mult))
                link(dve.tensor_tensor(tf, tf, tmp, ALU.add))
                dve.tensor_scalar(ang[:, 1, :], tf, pi, -pi, ALU.min, ALU.max).then_inc(s_cst, 1)
                norm1(0, 0)
                dve.wait_ge(s_tanh0, 1)
                sn, ta = g[:, 5, 0:64], g[:, 5, 64:128]
                link(dve.scalar_tensor_tensor(out=ta, in0=ta, scalar=1.0, in1=sn, op0=ALU.add, op1=ALU.mult))
                dve.tensor_scalar(g[:, 4, 64:128], ta, 0.5, None, ALU.mult).then_inc(s_emb, 1)
                apply1(0)
                dve.wait_ge(s_embmm, 1)
                for m in range(4):
                    link(dve.tensor_scalar(emb[:, m, :], M2[:, 0, m * B:(m + 1) * B], bad[:, m:m + 1],
                                           1.0 if m < 2 else 0.0, ALU.add, ALU.add))
                cur_copy(0, 0)
                link(dve.tensor_scalar(bqk[:, :, 0], bqk[:, :, 0], HD ** -0.5, None, ALU.mult))
                link(dve.tensor_scalar(b1s[:], b1c[:], GELU / 2, None, ALU.mult))
                dve.wait_ge(s_id, 3)
                dve.tensor_copy(ident_r[:], ident[:]).then_inc(s_split, 1)
                ring = PT[:].rearrange("p a t s -> p (a t s)")

                def split_weight(k, hl, raw):
                    dve.wait_ge(ld_w[k], 16)
                    link(dve.tensor_copy(hl[:, 0], raw))
                    return dve.tensor_tensor(hl[:, 1], raw, hl[:, 0].bitcast(F32), ALU.subtract)

                raws = [ring[:, k * NC * D:(k + 1) * NC * D].rearrange("p (k n) -> p k n", k=NC) for k in range(4)]
                split_weight(0, wq_hl, raws[0])
                x_split(0, 0)
                split_weight(1, wk_hl, raws[1]).then_inc(s_split, 1)
                split_weight(2, wv_hl, raws[2]).then_inc(s_split, 1)
                qk_split(0, 0)
                qk_split(0, 1)
                split_weight(3, wo_hl, raws[3]).then_inc(s_split, 1)
                split_weight(4, w1_hl, ring[:, 2048:4096].rearrange("p (k n) -> p k n", k=NC)).then_inc(s_split, 1)
                dve.wait_ge(ld_g, 16 * 6)
                for end in range(2):
                    sg = 1.0 if end == 0 else -1.0
                    for k, (cb, ca, c2_) in enumerate(((1.0, 1.5, -3.0), (-2.5, -2.0, 4.0), (2.0, 0.5, -1.0), (-0.5, 0.0, 0.0))):
                        o, k = (k, k) if end == 0 else (S - 1 - k, 3 - k)
                        link(dve.tensor_scalar(edge[:, :, end, k:k + 1], gR[:, :, o:o + 1], sg * ca, None, ALU.mult))
                        link(dve.scalar_tensor_tensor(out=edge[:, :, end, k:k + 1], in0=gC[:, :, o:o + 1], scalar=cb,
                                                      in1=edge[:, :, end, k:k + 1], op0=ALU.mult, op1=ALU.add))
                        link(dve.tensor_scalar(edge[:, :, 2 + end, k:k + 1], gB2[:, :, o:o + 1], sg * c2_, None, ALU.mult))
                link(dve.tensor_scalar(gA0, gA0, -2.0, None, ALU.mult))
                link(dve.tensor_tensor(gL, gC, gR, ALU.add))
                link(dve.tensor_tensor(gR, gC, gR, ALU.subtract))
                link(dve.tensor_scalar(gL, gL, 0.5, None, ALU.mult))
                link(dve.tensor_scalar(gR, gR, 0.5, None, ALU.mult))
                link(dve.tensor_scalar(gC, gC, -1.0, None, ALU.mult))

            def body(j, par, att, nxt, post, sten):
                i = j * 2 + par
                b = i - 1
                d = i - 2
                zero = isinstance(i, int) and i == 0
                first = isinstance(b, int) and b == 0
                dfirst = isinstance(d, int) and d == 0
                for n in range(H):
                    if att:
                        by_itself(dve, (s_S, i * H + n + 1), (s_madd, i * H + n + 1))
                        for t in range(NT):
                            dve.tensor_tensor_reduce(out=bias[:, n // GROUP, n % GROUP, t], in0=pS[n % 2][:, t],
                                                     in1=bias[:, n // GROUP, n % GROUP, t], scale=-1.0, scalar=HUGE,
                                                     op0=ALU.add, op1=ALU.min,
                                                     accum_out=nmax[:, n, t:t + 1]).then_inc(s_ttr, 1)
                    if n % 2 == 1:
                        if n >= 2 and att:
                            probs_evac(i, n - 2)
                        if n < 2 and post:
                            probs_evac(b, n - 2 + H)
                    if att and n == 3:
                        dve.wait_ge(s_v, i + 1)
                        if zero:
                            dve.wait_ge(s_zero, 3)
                        if not zero:
                            dve.wait_ge(s_ctx, i * NG)
                        for t in range(NT):
                            for e in range(2):
                                last = dve.tensor_tensor(
                                    V[:, t, e::2, HD * e:HD * e + HD],
                                    M0[:, t, :].rearrange("p (h e d) -> p h e d", e=2, d=HD)[:, :, e, :],
                                    bv_row[:].rearrange("p (h e d) -> p h e d", e=2, d=HD)[:, :, e, :], ALU.add)
                        last.then_inc(s_vev, 1)
                    if post and n == 1:
                        dve.wait_ge(s_exp, i * 32)
                        if not first:
                            dve.wait_ge(s_rbc, b)
                        dve.reciprocal(rec[:], sums[:, 1 - par]).then_inc(s_rec, 1)
                    if post and n == 3:
                        dve.wait_ge(s_ctx, i * NG)
                        dve.wait_ge(s_rTs, i)
                        if not first:
                            dve.wait_ge(s_x2b, b * 2)
                        dve.tensor_tensor(cn[:], pC_[:], rTs[:], ALU.mult).then_inc(s_cn, 1)
                        dve.wait_ge(s_cn, i)
                        dve.tensor_copy(cT[:, 0], cn[:]).then_inc(s_chi, 1)
                        dve.wait_ge(s_chi, i)
                        dve.tensor_tensor(cT[:, 1], cn[:], cT[:, 0].bitcast(F32), ALU.subtract).then_inc(s_chl, 1)
                    if sten:
                        if n == 0:
                            dve.wait_ge(s_x3, d + 1)
                            if not dfirst:
                                dve.wait_ge(stored, d * 16)
                            dve.tensor_tensor(pR[:], x3[:], gR, ALU.mult).then_inc(s_pRL, 1)
                            dve.tensor_tensor(pL[:], x3[:], gL, ALU.mult).then_inc(s_pRL, 1)
                            dve.wait_ge(s_pRL, (d + 1) * 2)
                            dve.tensor_tensor(tt[:, :, 1:S - 1], pR[:, :, 2:S], pL[:, :, 0:S - 2], ALU.add).then_inc(s_tt, 1)
                        if n == 1:
                            dve.wait_ge(s_tt, d * 3 + 1)
                            dve.tensor_tensor(pC[:], x3[:], gC, ALU.mult).then_inc(s_pC, 1)
                            for end in range(2):
                                f4 = x3[:, :, 0:4] if end == 0 else x3[:, :, S - 4:S]
                                for kind in range(2):
                                    dve.tensor_tensor(ed[:, :, 2 * kind + end, :], f4, edge[:, :, 2 * kind + end, :], ALU.mult)\
                                        .then_inc(s_ed, 1)
                            dve.wait_ge(s_pC, d + 1)
                            dve.tensor_tensor(tt[:, :, 1:S - 1], tt[:, :, 1:S - 1], pC[:, :, 1:S - 1], ALU.add).then_inc(s_tt, 1)
                            dve.wait_ge(s_ed, (d + 1) * 4)
                            dve.tensor_reduce(out=tt[:, :, 0:S:S - 1], in_=ed[:, :, 0:2, :], axis=AXES.X, op=ALU.add).then_inc(s_tt, 1)
                        if n == 2:
                            dve.wait_ge(s_b2f, d + 1)
                            dve.wait_ge(s_a0f, d + 1)
                            inner = u1[:, :, 1:S - 1]
                            dve.tensor_tensor(inner, inner, b2f[:, :, 2:S], ALU.add).then_inc(s_d1, 1)
                            dve.tensor_reduce(out=u1e[:], in_=ed[:, :, 2:4, :], axis=AXES.X, op=ALU.add).then_inc(s_d1, 1)
                            dve.wait_ge(s_d1, (d + 1) * 2)
                            dve.tensor_tensor(inner, inner, b2f[:, :, 0:S - 2], ALU.subtract).then_inc(s_u1, 1)
                            dve.tensor_tensor(u1[:, :, 0:S:S - 1], u1[:, :, 0:S:S - 1], u1e[:], ALU.add).then_inc(s_u1, 1)
                        if n == 4:
                            dve.wait_ge(s_st, d + 1)
                            dve.wait_ge(s_tt, (d + 1) * 3)
                            dve.tensor_tensor(yy[:], M2[:], tt[:], ALU.add).then_inc(s_y, 1)
                            dve.wait_ge(s_y, d + 1)
                            dve.wait_ge(s_dcur, d + 1)
                            dve.scalar_tensor_tensor(out=zf[:], in0=yy[:], scalar=dcur[:, 0:1], in1=x3[:],
                                                     op0=ALU.mult, op1=ALU.add).then_inc(s_zf, 1)
                    if nxt and n == 2:
                        norm1(i + 1, 1 - par)
                    if nxt and n == 3:
                        cur_copy(i + 1, 1 - par)
                    if nxt and n == 4:
                        apply1(i + 1)
                    if nxt and n == 6:
                        x_split(i + 1, 1 - par)
                    if post and n == 5:
                        dve.wait_ge(s_wo, i)
                        if not first:
                            dve.wait_ge(s_x2b, b * 2)
                        for t in range(NT):
                            dve.tensor_tensor(x2[:, t], M0[:, t], bo_row[:], ALU.add).then_inc(s_x2, 1)
                        dve.wait_ge(s_x2, i * 2)
                        norm(b, x2, stat2, mv2, s_stat2, s_mv2)
                    if post and n == 6:
                        dve.wait_ge(s_rs2, i)
                        if nxt:
                            dve.wait_ge(s_xT, i + 2)
                        apply_norm(hn, x2, mv2, rs2, s_hn)
                    if post and n == 7:
                        dve.wait_ge(s_hTf, i * 2)
                        dve.tensor_copy(hT[:, 0], hTf[:]).then_inc(s_hhi, 1)
                        dve.wait_ge(s_hhi, i)
                        dve.tensor_tensor(hT[:, 1], hTf[:], hT[:, 0].bitcast(F32), ALU.subtract).then_inc(s_hhl, 1)
                    if nxt and n == 8:
                        qk_split(i + 1, 0)
                    if post and 8 <= n < 12:
                        f = n - 8
                        dve.wait_ge(s_tanh, b * 8 + 2 * f + 2)
                        if f == 0 and not first:
                            dve.wait_ge(s_f2, b)
                        for m in range(2):
                            dve.tensor_scalar(g[:, 2 * f + m], (M0, M1)[f % 2][:, m], b1c[:, 2 * f + m:2 * f + m + 1],
                                              None, ALU.add).then_inc(s_z, 1)
                        dve.wait_ge(s_z, b * 8 + 2 * f + 2)
                        dve.scalar_tensor_tensor(out=g[:, 2 * f:2 * f + 2], in0=th[:, f % 2], scalar=1.0,
                                                 in1=g[:, 2 * f:2 * f + 2], op0=ALU.add, op1=ALU.mult).then_inc(s_g, 1)
                    if nxt and n == 13:
                        qk_split(i + 1, 1)
                    if post and n == 15:
                        dve.wait_ge(s_f2, i)
                        dve.wait_ge(s_x2b, i * 2)
                        if not first:
                            dve.wait_ge(s_zf, b)
                        dve.tensor_copy(dcur[:], dt_row[:, column(b)]).then_inc(s_dcur, 1)
                        dve.scalar_tensor_tensor(out=x3[:], in0=M2[:], scalar=0.5, in1=x2b[:],
                                                 op0=ALU.mult, op1=ALU.add).then_inc(s_x3, 1)

            run(dve, prologue, body)


def _stencil_matrices(np):
    m = np.zeros((2, S, S), np.float32)
    for k in range(1, S - 1):
        m[0, k + 1, k], m[0, k - 1, k] = 0.25, -0.25
        m[1, k + 1, k], m[1, k, k], m[1, k - 1, k] = 0.5, -1.0, 0.5
    m[0, 0:3, 0] = (-0.75, 1.0, -0.25)
    m[0, S - 3:, S - 1] = (0.25, -1.0, 0.75)
    m[1, 0:4, 0] = (1.0, -2.5, 2.0, -0.5)
    m[1, S - 4:, S - 1] = (-0.5, 2.0, -2.5, 1.0)
    return m


def kernel(**inputs):
    import numpy as np
    import concourse.bacc as bacc
    from concourse.bass_utils import run_bass_kernel_spmd

    def stacked(w):
        w = np.asarray(w)
        return w.reshape(-1, NC, 4, 2, HD).transpose(0, 1, 3, 4, 2).reshape(w.shape)

    given = {k: np.asarray(v) for k, v in inputs.items()}
    layer = lambda name: given["L0_cond_" + name]
    arrays = {
        "x": given["x"], "itok": given["itok_B_34_63"], "fside": given["fside_Bx16xSxS_0"], "dt": given["condB_dt"],
        "mask": given["mask_Bx1xSxS_bk0"].view(np.int32).reshape(B, S, S // 4),
        "W_ada": layer("W_ada"), "b_ada": layer("b_ada"),
        "Wq": stacked(layer("Wq")), "bq": stacked(layer("bq")), "Wk": stacked(layer("Wk")), "bk": stacked(layer("bk")),
        "Wv": layer("Wv"), "bv": layer("bv"), "Wo": layer("Wo"), "bo": layer("bo"),
        "W1": layer("W1"), "b1": layer("b1"), "W2": layer("W2"), "b2": layer("b2"),
        "g2": layer("g2"), "beta2": layer("beta2"),
        "A_grid": given["L1_cond_A_grid"], "B_grid": given["L1_cond_B_grid"],
        "freqs": np.exp(np.arange(P, dtype=np.float32) * np.float32(-np.log(10000.0) / (P - 1))),
        "stencils": _stencil_matrices(np),
    }
    nc = bacc.Bacc("TRN2", target_bir_lowering=False, num_devices=1)
    args = []
    for name, a in arrays.items():
        arrays[name] = a = np.ascontiguousarray(a)
        args.append(nc.dram_tensor(name, a.shape, mybir.dt.from_np(a.dtype), kind="ExternalInput").ap())
    out = nc.dram_tensor("out", (B, S, D), F32, kind="ExternalOutput").ap()
    order = ["x", "itok", "fside", "dt", "mask", "W_ada", "b_ada", "Wq", "bq", "Wk", "bk", "Wv", "bv", "Wo", "bo",
             "W1", "b1", "W2", "b2", "g2", "beta2", "A_grid", "B_grid", "freqs", "stencils"]
    named = dict(zip(arrays, args))
    build(nc, *[named[n] for n in order], out)
    result = run_bass_kernel_spmd(nc, [arrays], core_ids=[0])
    return result.results[0]["out"]
```

```python
import concourse.bass as bass
from concourse import mybir
from contextlib import ExitStack

ALU = mybir.AluOpType
ACT = mybir.ActivationFunctionType
AXES = mybir.AxisListType
F32 = mybir.dt.float32
F32R = mybir.dt.float32r
BF16 = mybir.dt.bfloat16
I32 = mybir.dt.int32
U8 = mybir.dt.uint8

B, S, D, H, HD, FF = 32, 256, 256, 16, 16, 1024
P = 128
NT = S // P
NC = D // P
NF = FF // P
GROUP = 4
NG = H // GROUP
ROWS = 64
PARTS = 3
P_RING, PT_RING = 4, 8
EPS = 1e-5
NEG = -2.0 ** 127
HUGE = 3.4e38
GELU = 1.702


AT_SP = {"src": 5, "mask": 1, "scatter": [5, 20], "bias": [13, 18, 18, 24], "store": 25}
AT_POOL = {"power1": 14, "mask": 24, "power2": 15, "x2b": 31, "one_plus_tanh": [20, 24, 25, 26],
           "products": 1, "u1": 4, "u2": 2, "sides": 4, "side_sum": 17, "centre_sum": 18}
AT_PE = {"x.T": 14, "qk": [19, 31], "v": 2, "rec.T": 2, "rec spread": 4, "wo": 12,
         "h.T": 19, "ffn1": [23, 24, 27, 28], "ffn2": [30, 31, 31, 31], "stencil": 8}
AT_ACT = {"x.T": 13, "qk": [19, 31], "rec.T": 1, "rec spread": 4, "h.T": 17,
          "tanh": [21, 23, 24, 27], "relu": 25}
AT_DVE = {"norm1": 9, "x": 11, "x split": 15, "qk split": [21, 31], "v": 5, "rec": 0,
          "context": 5, "x2": 13, "h": 16, "h split": 20, "gelu": [25, 26, 30, 30],
          "edges": 4, "edge sums": 4, "z": 28, "x3": 31}
PT_ON_ACT = (0,)


def head_of(n):
    c, e, j = n // 8, (n // 4) % 2, n % 4
    return 8 * c + 2 * j + e


def build(nc, x, itok, fside, dt, mask, W_ada, b_ada, Wq, bq, Wk, bk, Wv, bv, Wo, bo, W1, b1, W2, b2,
          g2, beta2, A_grid, B_grid, freqs, stencils, selector, out):
    ctx = ExitStack()
    with ctx:
        def sb(name, shape, dtype=F32):
            return ctx.enter_context(nc.sbuf_tensor(name, shape, dtype))

        def sem(name):
            return ctx.enter_context(nc.semaphore(name))

        ident = sb("ident", [P, P])
        ident_r = sb("ident_r", [P, P], F32R)
        ident_b = sb("ident_b", [P, P], BF16)
        wq_hl = sb("wq_hl", [P, 2, NC, D], F32R)
        wk_hl = sb("wk_hl", [P, 2, NC, D], F32R)
        wv_hl = sb("wv_hl", [P, 2, NC, D], F32R)
        wo_hl = sb("wo_hl", [P, 2, NC, D], F32R)
        w1_hl = sb("w1_hl", [P, 2, NC, FF], F32R)
        w2 = sb("w2", [P, NF, D])
        sten_w = sb("sten_w", [P, 2, NT, S])
        bqk = sb("bqk", [P, NC, 2])
        b1c = sb("b1c", [P, NF])
        b1s = sb("b1s", [P, NF])
        g2c = sb("g2c", [P, NC])
        be2c = sb("be2c", [P, NC])
        bv_row = sb("bv_row", [P, D])
        bo_row = sb("bo_row", [P, D])
        b2_row = sb("b2_row", [P, D])
        half = sb("half", [P, NT])
        emb = sb("emb", [P, 4, B])
        dt_row = sb("dt_row", [P, B])
        grids = sb("grids", [P, 6, NT, D])
        gA0, gB0, gR, gL, gC, gB2 = (grids[:, k] for k in range(6))
        edge = sb("edge", [P, NT, 4, 4])

        bias = sb("bias", [P, NG, GROUP, NT, S])
        mask_w = sb("mask_w", [P, NT, S // 4], I32)
        mneg = sb("mneg", [P, 2, NT, S], BF16)
        src = sb("src", [P, NT, D])
        xn = sb("xn", [P, NT, D])
        xTf = sb("xTf", [P, NC, S])
        xT = sb("xT", [P, 2, 2, NC, S], F32R)
        cur = sb("cur", [P, 2, 4])
        dcur = sb("dcur", [P, 1])
        bad = sb("bad", [P, 4])
        qkf = xTf
        qk = sb("qk", [P, 2, 2, S], F32R)
        Qs = sb("Qs", [P, H // 2, S], F32R)
        Ks = sb("Ks", [P, H, S], F32R)
        V = sb("V", [P, NT, H, 32])
        nmax = sb("nmax", [P, H, NT])
        Pb = sb("Pb", [P, P_RING, NT, S])
        PT = sb("PT", [P, PT_RING, NT, S])
        sums = sb("sums", [P, 2, NT, H])
        rec = sb("rec", [P, NT, H])
        recT = sb("recT", [H, S])
        sel = sb("sel", [H, NC, P])
        cT = sb("cT", [P, 2, NC, S], F32R)
        stat1 = sb("stat1", [P, NT, 6])
        mv1 = sb("mv1", [P, NT, 2])
        ve1 = sb("ve1", [P, NT])
        rs1 = sb("rs1", [P, NT])
        stat2 = sb("stat2", [P, NT, 6])
        mv2 = sb("mv2", [P, NT, 2])
        ve2 = sb("ve2", [P, NT])
        rs2 = sb("rs2", [P, NT])
        x2 = sb("x2", [P, NT, D])
        cn = x2
        x2b = sb("x2b", [P, NT, D])
        hn = xn
        hTf = sb("hTf", [P, NC, S])
        rTs = hTf
        hT = sb("hT", [P, 2, NC, S], F32R)
        th = sb("th", [P, 2, 2, S])
        g = sb("g", [P, NF, S])
        x3 = sb("x3", [P, NT, D])
        pR = sb("pR", [P, NT, D])
        pL = sb("pL", [P, NT, D])
        pC = pR
        tt = sb("tt", [P, NT, D])
        b2f = x2b
        a0f = sb("a0f", [P, NT, D])
        u1 = a0f
        u1e = sb("u1e", [P, NT, 2])
        u2 = sb("u2", [P, NT, D])
        ed = sb("ed", [P, NT, 4, 4])
        yy = tt
        zf = pL

        def bank(name, shape):
            return ctx.enter_context(nc.psum_tensor(name, shape, F32))

        pS = [bank(f"pS{k}", [P, NT, S]) for k in range(2)]
        pT = [bank(f"pT{k}", [P, NT, S]) for k in range(2)]
        pC_ = bank("pCtx", [P, NC, S])
        M0 = bank("M0", [P, 2, S])
        M1 = bank("M1", [P, 2, S])
        M2 = bank("M2", [P, NT, D])

        ld_w = [sem(f"ld_w{k}") for k in range(6)]
        ld_c = sem("ld_c")
        ld_g = sem("ld_g")
        ld_w2 = sem("ld_W2")
        ld_src = sem("ld_src")
        ld_mask = sem("ld_mask")
        ld_bias = [sem(f"ld_bias{k}") for k in range(NG)]
        scat = [sem(f"scat{c}") for c in range(NC)]
        stored = sem("stored")
        s_id = sem("s_id")
        s_cst = sem("s_cst")
        s_emb = sem("s_emb")
        s_sin = sem("s_sin")
        s_embmm = sem("s_embmm")
        s_tanh0 = sem("s_tanh0")
        s_split = sem("s_split")
        s_stat1 = sem("s_stat1"); s_mv1 = sem("s_mv1"); s_ve1 = sem("s_ve1"); s_rs1 = sem("s_rs1")
        s_stat2 = sem("s_stat2"); s_mv2 = sem("s_mv2"); s_ve2 = sem("s_ve2"); s_rs2 = sem("s_rs2")
        s_cur = sem("s_cur"); s_dcur = sem("s_dcur"); s_lnk = sem("s_lnk")
        s_xn = sem("s_xn"); s_xT = sem("s_xT"); s_xTf = sem("s_xTf"); s_xhi = sem("s_xhi"); s_xhl = sem("s_xhl")
        s_qk = sem("s_qk"); s_qkf = sem("s_qkf"); s_qhi = sem("s_qhi"); s_qhl = sem("s_qhl")
        s_zero = sem("s_zero")
        s_v = sem("s_v"); s_vev = sem("s_vev")
        s_mneg = sem("s_mneg")
        s_S = sem("s_S"); s_ttr = sem("s_ttr"); s_exp = sem("s_exp")
        s_T = sem("s_T"); s_ptA = sem("s_ptA"); s_ptD = sem("s_ptD"); s_ctx = sem("s_ctx")
        s_rec = sem("s_rec"); s_recT = sem("s_recT"); s_recTs = sem("s_recTs"); s_rT = sem("s_rT"); s_rTs = sem("s_rTs")
        s_cn = sem("s_cn"); s_chi = sem("s_chi"); s_chl = sem("s_chl")
        s_wo = sem("s_wo"); s_x2 = sem("s_x2"); s_x2b = sem("s_x2b"); s_hn = sem("s_hn")
        s_hT = sem("s_hT"); s_hTf = sem("s_hTf"); s_hhi = sem("s_hhi"); s_hhl = sem("s_hhl")
        s_f1 = sem("s_f1"); s_tanh = sem("s_tanh"); s_th1 = sem("s_th1"); s_g = sem("s_g")
        s_f2 = sem("s_f2"); s_x3 = sem("s_x3")
        s_b2f = sem("s_b2f"); s_a0f = sem("s_a0f"); s_u2 = sem("s_u2")
        s_pRL = sem("s_pRL"); s_tt = sem("s_tt"); s_pC = sem("s_pC"); s_ed = sem("s_ed")
        s_d1 = sem("s_d1"); s_u1 = sem("s_u1"); s_e1 = sem("s_e1"); s_u1e = sem("s_u1e"); s_te = sem("s_te")
        s_st = sem("s_st"); s_y = sem("s_y"); s_zf = sem("s_zf"); s_relu = sem("s_relu")

        FULL = dict(att=True, nxt=True, post=True, sten=True)

        def run(eng, prologue, body):
            prologue()
            body(0, 0, att=True, nxt=True, post=False, sten=False)
            body(0, 1, att=True, nxt=True, post=True, sten=False)
            with eng.Fori(1, B // 2 - 1) as j:
                body(j, 0, **FULL)
                body(j, 1, **FULL)
            body(B // 2 - 1, 0, **FULL)
            body(B // 2 - 1, 1, att=True, nxt=False, post=True, sten=True)
            body(B // 2, 0, att=False, nxt=False, post=True, sten=True)
            body(B // 2, 1, att=False, nxt=False, post=False, sten=True)

        def by_itself(eng, *waits):
            for _, v in waits:
                eng.compute_val(v)
            eng.wait_ge(s_id, 3)
            for s_, v in waits:
                eng.wait_ge(s_, v)

        block = ctx.enter_context(nc.Block())

        @block.sync
        def _(sp):
            def tok(ap):
                return ap.rearrange("(t p) n -> p t n", p=P)

            def at(ap, i):
                return ap[i] if isinstance(i, int) else ap[bass.ds(i, 1)].rearrange("o a n -> (o a) n")

            def load_src(i):
                sp.dma_start(src[:], tok(at(x, i))).then_inc(ld_src, 16)

            def load_mask(i):
                sp.dma_start(mask_w[:], tok(at(mask, i))).then_inc(ld_mask, 16)

            def load_bias(i, n):
                c, e = n // 2, n % 2
                for t in range(NT):
                    rows = (fside[i] if isinstance(i, int) else
                            fside[bass.ds(i, 1)].rearrange("o h q k -> (o h) q k"))
                    part = rows[8 * c + e:8 * c + 8:2, t * P:(t + 1) * P, :].rearrange("h p k -> p h k")
                    sp.dma_start(bias[:, n, :, t, :], part).then_inc(ld_bias[n], 16)

            def scatter(c):
                for s in range(2):
                    for r in range(PARTS):
                        for w, high_low in ((0, (0, 1, 0)), (1, (0, 0, 1))):
                            rows = slice(ROWS * s + HD * r, ROWS * s + HD * (r + 1))
                            into = Qs[rows, 4 * c:4 * c + 4, :] if w == 0 else Ks[rows, 8 * c + s:8 * c + 8:2, :]
                            sp.dma_start(into.bitcast(F32), qk[64 * s:64 * s + 64, high_low[r], w, :].bitcast(F32))\
                              .then_inc(scat[c], 16)

            def prologue():
                load_src(0)
                small = [(b_ada.rearrange("(m p) -> p m", p=P), emb[:, 0, 0:4]),
                         (freqs.rearrange("(p o) -> p o", o=1), emb[:, 0, 4:5]),
                         (bq.rearrange("(c p) -> p c", p=P), bqk[:, :, 0]),
                         (bk.rearrange("(c p) -> p c", p=P), bqk[:, :, 1]),
                         (b1.rearrange("(m p) -> p m", p=P), b1c[:]),
                         (g2.rearrange("(c p) -> p c", p=P), g2c[:]),
                         (beta2.rearrange("(c p) -> p c", p=P), be2c[:])]
                with nc.allow_non_contiguous_dma(reason="small vectors, once"):
                    for from_, into in small:
                        sp.dma_start(into, from_).then_inc(ld_c, 16)
                for from_, into in ((bv, bv_row), (bo, bo_row), (b2, b2_row), (dt, dt_row)):
                    sp.dma_start(into[:], from_.partition_broadcast(P)).then_inc(ld_c, 16)
                sp.dma_start(sel[:], selector).then_inc(ld_c, 16)
                sp.dma_start(th[:, 0, 0, 0:B].bitcast(I32),
                             itok.partition_broadcast(P)).then_inc(ld_c, 16)
                ring = PT[:].rearrange("p a t s -> p (a t s)")
                sp.dma_start(g[:, 0:4, :].rearrange("p a b -> p (a b)").rearrange("p (k n) -> p k n", k=2),
                             W_ada.rearrange("(k p) n -> p k n", p=P)).then_inc(ld_w[5], 16)
                for k, w in enumerate((Wq, Wk, Wv, Wo)):
                    sp.dma_start(ring[:, k * NC * D:(k + 1) * NC * D].rearrange("p (k n) -> p k n", k=NC),
                                 w.rearrange("(k p) n -> p k n", p=P)).then_inc(ld_w[k], 16)
                load_mask(0)
                load_bias(0, 0)
                sp.dma_start(ring[:, 2048:4096].rearrange("p (k n) -> p k n", k=NC),
                             W1.rearrange("(k p) n -> p k n", p=P)).then_inc(ld_w[4], 16)
                for n in range(1, NG):
                    load_bias(0, n)
                sp.dma_start(w2[:], W2.rearrange("(k p) n -> p k n", p=P)).then_inc(ld_w2, 16)
                for g_, into in ((A_grid[0], gA0), (B_grid[0], gB0), (A_grid[1], gR), (B_grid[1], gC), (B_grid[2], gB2)):
                    sp.dma_start(into, tok(g_)).then_inc(ld_g, 16)
                sp.dma_start(sten_w[:], stencils.rearrange("m (k p) n -> p m k n", p=P)).then_inc(ld_g, 16)
                for c in range(NC):
                    if c == 0:
                        sp.wait_ge(s_zero, 2)
                    sp.wait_ge(s_qhl, c + 1)
                    scatter(c)

            def body(j, par, att, nxt, post, sten):
                i = j * 2 + par
                for h in range(2 * H):
                    if nxt and h == AT_SP["src"]:
                        by_itself(sp, (s_xn, (i + 1) * 2))
                        load_src(i + 1)
                    if nxt and h == AT_SP["mask"]:
                        by_itself(sp, (s_mneg, i + 1))
                        load_mask(i + 1)
                    for c in range(NC):
                        if nxt and h == AT_SP["scatter"][c]:
                            by_itself(sp, (s_qhl, (i + 1) * 2 + c + 1), (s_S, i * H + 8 * c + 8))
                            scatter(c)
                    for gr in range(NG):
                        if nxt and h == AT_SP["bias"][gr]:
                            by_itself(sp, (s_exp, i * 32 + 8 * gr + 8))
                            load_bias(i + 1, gr)
                    if sten and h == AT_SP["store"]:
                        by_itself(sp, (s_relu, i - 1))
                        sp.dma_start(tok(at(out, i - 2)), zf[:]).then_inc(stored, 16)

            run(sp, prologue, body)
            sp.wait_ge(stored, 16 * B)

        @block.gpsimd
        def _(pool):
            def mask_values(i, par):
                waits = [(ld_mask, i * 16 + 16)]
                if not (isinstance(i, int) and i < 2):
                    waits.append((s_S, (i - 1) * H))
                by_itself(pool, *waits)
                pool.tensor_scalar(mneg[:, par], mask_w[:].bitcast(U8), NEG, 1.0, ALU.mult, ALU.mult).then_inc(s_mneg, 1)

            def power(mv, ve, rs, s_mv, s_ve, s_rs, i):
                by_itself(pool, (s_mv, (i + 1) * 2))
                pool.tensor_scalar(ve[:], mv[:, :, 1], EPS, 1.0, ALU.add, ALU.mult).then_inc(s_ve, 1)
                pool.wait_ge(s_ve, i + 1)
                pool.tensor_tensor(rs[:], ve[:], half[:], ALU.pow).then_inc(s_rs, 1)

            def prologue():
                pool.memset(ident[:], 0.0).then_inc(s_id, 1)
                pool.memset(half[:], -0.5).then_inc(s_id, 1)
                pool.wait_ge(s_id, 2)
                pool.affine_select(out=ident[:], in_=ident[:], compare_op=ALU.not_equal, fill=1.0, base=0,
                                   pattern=[[-1, P]], channel_multiplier=1).then_inc(s_id, 1)
                power(mv1, ve1, rs1, s_mv1, s_ve1, s_rs1, 0)
                pool.memset(Ks[:].bitcast(F32), 0.0).then_inc(s_zero, 1)
                pool.memset(Qs[:].bitcast(F32), 0.0).then_inc(s_zero, 1)
                pool.memset(V[:], 0.0).then_inc(s_zero, 1)
                mask_values(0, 0)

            def body(j, par, att, nxt, post, sten):
                i = j * 2 + par
                b, d = i - 1, i - 2
                first = isinstance(b, int) and b == 0
                dfirst = isinstance(d, int) and d == 0
                u_in, t_in = u1[:, :, 1:S - 1], tt[:, :, 1:S - 1]
                for h in range(2 * H):
                    if nxt and h == AT_POOL["power1"]:
                        power(mv1, ve1, rs1, s_mv1, s_ve1, s_rs1, i + 1)
                    if nxt and h == AT_POOL["mask"]:
                        mask_values(i + 1, 1 - par)
                    if post and h == AT_POOL["power2"]:
                        power(mv2, ve2, rs2, s_mv2, s_ve2, s_rs2, b)
                    if post and h == AT_POOL["x2b"]:
                        pool.wait_ge(s_x2, i * 2)
                        if not first:
                            pool.wait_ge(s_x3, b)
                        if sten:
                            pool.wait_ge(s_u1, d + 1)
                        for t in range(NT):
                            pool.tensor_tensor(x2b[:, t], x2[:, t], b2_row[:], ALU.add).then_inc(s_x2b, 1)
                    for f in range(NF // 2):
                        if post and h == AT_POOL["one_plus_tanh"][f]:
                            by_itself(pool, (s_tanh, b * 8 + 2 * f + 2))
                            pool.tensor_scalar(th[:, f % 2], th[:, f % 2], 1.0, 1.0, ALU.add, ALU.mult).then_inc(s_th1, 1)
                    if sten and h == AT_POOL["products"]:
                        pool.wait_ge(s_x3, d + 1)
                        if not dfirst:
                            pool.wait_ge(s_st, d)
                        pool.tensor_tensor(a0f[:], x3[:], gA0, ALU.mult).then_inc(s_a0f, 1)
                        pool.tensor_tensor(b2f[:], x3[:], gB2, ALU.mult).then_inc(s_b2f, 1)
                    if sten and h == AT_POOL["u1"]:
                        pool.wait_ge(s_a0f, d + 1)
                        pool.wait_ge(s_b2f, d + 1)
                        pool.tensor_tensor(u_in, u_in, b2f[:, :, 2:S], ALU.add).then_inc(s_d1, 1)
                        pool.wait_ge(s_d1, d + 1)
                        pool.tensor_tensor(u_in, u_in, b2f[:, :, 0:S - 2], ALU.subtract).then_inc(s_u1, 1)
                    if sten and h == AT_POOL["u2"]:
                        if not dfirst:
                            pool.wait_ge(s_st, d)
                        pool.tensor_tensor(u2[:], x3[:], gB0, ALU.mult).then_inc(s_u2, 1)
                    if sten and h == AT_POOL["sides"]:
                        if not dfirst:
                            pool.wait_ge(s_tt, d * 2)
                        pool.tensor_tensor(pR[:], x3[:], gR, ALU.mult).then_inc(s_pRL, 1)
                        if not dfirst:
                            pool.wait_ge(stored, d * 16)
                        pool.tensor_tensor(pL[:], x3[:], gL, ALU.mult).then_inc(s_pRL, 1)
                    if sten and h == AT_POOL["side_sum"]:
                        pool.wait_ge(s_pRL, (d + 1) * 2)
                        if not dfirst:
                            pool.wait_ge(s_zf, d)
                        pool.tensor_tensor(t_in, pR[:, :, 2:S], pL[:, :, 0:S - 2], ALU.add).then_inc(s_tt, 1)
                        pool.wait_ge(s_tt, d * 2 + 1)
                        pool.tensor_tensor(pC[:], x3[:], gC, ALU.mult).then_inc(s_pC, 1)
                    if sten and h == AT_POOL["centre_sum"]:
                        pool.wait_ge(s_pC, d + 1)
                        pool.tensor_tensor(t_in, t_in, pC[:, :, 1:S - 1], ALU.add).then_inc(s_tt, 1)

            run(pool, prologue, body)

        @block.tensor
        def _(pe):
            mm = nc.tensor.matmul

            def split_mm(into, lhs, rhs, k, nk, close=True):
                for m, (a, b) in enumerate(((0, 0), (1, 0), (0, 1))):
                    last = mm(into, lhs[a], rhs[b], start=(k == 0 and m == 0),
                              stop=(close and k == nk - 1 and m == 2))
                return last

            def transposes(into, from_):
                for c in range(2):
                    for t in range(2):
                        last = nc.tensor.transpose(into[:, c, t * P:(t + 1) * P], from_(t, c), ident[:])
                return last

            def x_transposed(i):
                pe.wait_ge(s_xn, (i + 1) * 2)
                transposes(M1, lambda t, c: xn[:, t, c * P:(c + 1) * P]).then_inc(s_xT, 1)

            def qk_product(i, par, c, M):
                for w, wt in ((0, wq_hl), (1, wk_hl)):
                    for k in range(NC):
                        last = split_mm(M[:, w, :], [wt[:, a, k, c * P:(c + 1) * P] for a in (0, 1)],
                                        [xT[:, par, a, k, :] for a in (0, 1)], k, NC)
                last.then_inc(s_qk, 1)

            def scores(i, par, n):
                if n % 8 == 0:
                    pe.wait_ge(scat[n // 8], (i + 1) * (16 * 4 * PARTS))
                if n == 0:
                    pe.wait_ge(s_mneg, i + 1)
                if n >= 2 or not (isinstance(i, int) and i == 0):
                    pe.wait_ge(s_ttr, i * 32 + 2 * n - 2)
                hd = head_of(n)
                for t in range(NT):
                    mm(pS[n % 2][:, t, :], Qs[:, hd // 2, t * P:(t + 1) * P], Ks[:, hd, :], start=True, stop=False)
                    last = mm(pS[n % 2][:, t, :], ident_b[:], mneg[:, par, t, :], start=False, stop=True)
                last.then_inc(s_S, 1)

            def transposed_probs(i, n):
                pe.wait_ge(s_exp, i * 32 + 2 * n + 2)
                if n >= 2 or not (isinstance(i, int) and i == 0):
                    pe.wait_ge(s_ptD if n % 2 else s_ptA, i * 8 + n // 2)
                for k in range(NT):
                    for t in range(NT):
                        last = nc.tensor.transpose(pT[n % 2][:, k, t * P:(t + 1) * P],
                                                   Pb[:, n % P_RING, t, k * P:(k + 1) * P], ident[:])
                last.then_inc(s_T, 1)

            def context(i, par, gr):
                pe.wait_ge(s_ptA, i * 8 + 2 * gr + 2)
                pe.wait_ge(s_ptD, i * 8 + 2 * gr + 2)
                if gr == 0:
                    pe.wait_ge(s_vev, i + 1)
                    if not (isinstance(i, int) and i == 0):
                        pe.wait_ge(s_cn, i)
                c, e = gr // 2, gr % 2
                for k in range(NT):
                    for q in range(GROUP):
                        n = gr * GROUP + q
                        last = mm(pC_[32 * q:32 * q + 32, c, :], V[:, k, head_of(n), :],
                                  PT[:, n % PT_RING, k, :], start=(e == 0 and k == 0),
                                  stop=(e == 1 and k == NT - 1))
                last.then_inc(s_ctx, 1)

            def prologue():
                pe.wait_ge(s_emb, 1)
                pe.wait_ge(ld_w[5], 16)
                wa = g[:, 0:4, :].rearrange("p a b -> p (a b)").rearrange("p (k n) -> p k n", k=2)
                silu = g[:, 4, 64:128].rearrange("p (k b) -> p k b", k=2)
                for m in range(4):
                    for k in range(2):
                        last = mm(M2[:, 0, m * B:(m + 1) * B], wa[:, k, m * P:(m + 1) * P], silu[:, k, :],
                                  start=(k == 0), stop=(k == 1))
                last.then_inc(s_embmm, 1)
                pe.wait_ge(s_id, 3)
                x_transposed(0)
                pe.wait_ge(s_split, 2)
                pe.wait_ge(s_xhl, 1)
                qk_product(0, 0, 0, M1)
                qk_product(0, 0, 1, M0)

            def body(j, par, att, nxt, post, sten):
                i = j * 2 + par
                b = i - 1
                zero = isinstance(i, int) and i == 0
                first = isinstance(b, int) and b == 0
                for h in range(2 * H):
                    n = h // 2
                    if h % 2 == 0 and att:
                        scores(i, par, n)
                    if h % 2 == 1:
                        if n >= 2 and att:
                            transposed_probs(i, n - 2)
                        if n < 2 and post:
                            transposed_probs(b, n - 2 + H)
                        gr = n // GROUP - 1
                        if n % GROUP == 2 and gr >= 0 and att:
                            context(i, par, gr)
                        if n % GROUP == 2 and gr < 0 and post:
                            context(b, 1 - par, NG - 1)
                    if nxt and h == AT_PE["x.T"]:
                        if post:
                            pe.wait_ge(s_rTs, i)
                        x_transposed(i + 1)
                    if nxt and h == AT_PE["qk"][0]:
                        pe.wait_ge(s_xhl, i + 2)
                        qk_product(i + 1, 1 - par, 0, M1)
                    if nxt and h == AT_PE["qk"][1]:
                        if post:
                            pe.wait_ge(s_g, b * 4 + 3)
                        qk_product(i + 1, 1 - par, 1, M0)
                    if att and h == AT_PE["v"]:
                        if zero:
                            pe.wait_ge(s_split, 4)
                        pe.wait_ge(s_qkf, (i + 1) * 4)
                        for t in range(NT):
                            for k in range(NC):
                                last = split_mm(M0[:, t, :], [xT[:, par, a, k, t * P:(t + 1) * P] for a in (0, 1)],
                                                [wv_hl[:, a, k, :] for a in (0, 1)], k, NC)
                        last.then_inc(s_v, 1)
                    if post and h == AT_PE["rec.T"]:
                        if not first:
                            pe.wait_ge(s_g, b * 4)
                        pe.wait_ge(s_rec, i)
                        for t in range(NT):
                            last = nc.tensor.transpose(M1[0:H, 0, t * P:(t + 1) * P], rec[:, t, :], ident[:])
                        last.then_inc(s_recT, 1)
                    if post and h == AT_PE["rec spread"]:
                        pe.wait_ge(s_recTs, i)
                        for c in range(NC):
                            last = mm(M1[:, c, :], sel[:, c, :], recT[:], start=True, stop=True)
                        last.then_inc(s_rT, 1)
                    if post and h == AT_PE["wo"]:
                        if att:
                            pe.wait_ge(s_vev, i + 1)
                        pe.wait_ge(s_chl, i)
                        for t in range(NT):
                            for k in range(NC):
                                split_mm(M0[:, t, :], [cT[:, a, k, t * P:(t + 1) * P] for a in (0, 1)],
                                         [wo_hl[:, a, k, :] for a in (0, 1)], k, NC, close=False)
                            for c in range(NC):
                                for a in (0, 1):
                                    last = mm(M0[:, t, c * P:(c + 1) * P], xT[:, 1 - par, a, c, t * P:(t + 1) * P],
                                              ident_r[:], start=False, stop=(c == NC - 1 and a == 1))
                        last.then_inc(s_wo, 1)
                    if post and h == AT_PE["h.T"]:
                        pe.wait_ge(s_hn, i * 2)
                        transposes(M0, lambda t, c: hn[:, t, c * P:(c + 1) * P]).then_inc(s_hT, 1)
                    for f in range(NF // 2):
                        if post and h == AT_PE["ffn1"][f]:
                            M = (M0, M1)[f % 2]
                            if f == 0:
                                pe.wait_ge(s_hhl, i)
                            if f == 1 and nxt:
                                pe.wait_ge(s_qkf, (i + 1) * 4 + 2)
                            if f >= 2:
                                pe.wait_ge(s_g, b * 4 + f - 1)
                            for m in range(2):
                                for k in range(NC):
                                    last = split_mm(M[:, m, :],
                                                    [w1_hl[:, a, k, (2 * f + m) * P:(2 * f + m + 1) * P] for a in (0, 1)],
                                                    [hT[:, a, k, :] for a in (0, 1)], k, NC)
                            last.then_inc(s_f1, 1)
                    for q in range(4):
                        if post and h == AT_PE["ffn2"][q]:
                            t, part = q // 2, q % 2
                            if q == 0 and sten:
                                pe.wait_ge(s_y, i - 1)
                            if q == 0 and first:
                                pe.wait_ge(ld_w2, 16)
                            pe.wait_ge(s_g, b * 4 + 2 * part + 2)
                            for f in range(4 * part, 4 * part + 4):
                                last = mm(M2[:, t, :], g[:, f, t * P:(t + 1) * P], w2[:, f, :],
                                          start=(f == 0), stop=(f == NF - 1))
                            if q == 3:
                                last.then_inc(s_f2, 1)
                    if sten and h == AT_PE["stencil"]:
                        pe.wait_ge(s_u1, i - 1)
                        pe.wait_ge(s_u1e, i - 1)
                        pe.wait_ge(s_u2, i - 1)
                        pe.wait_ge(s_x3, i - 1)
                        for t in range(NT):
                            for m, u in enumerate((u1, u2)):
                                for k in range(NT):
                                    last = mm(M2[:, t, :], sten_w[:, m, k, t * P:(t + 1) * P], u[:, k, :],
                                              start=(m == 0 and k == 0), stop=(m == 1 and k == NT - 1))
                        last.then_inc(s_st, 1)

            run(pe, prologue, body)

        @block.scalar
        def _(act):
            ident_f = ACT.Identity

            def x_evac(i, par):
                act.wait_ge(s_xT, i + 1)
                act.wait_ge(s_cur, i + 1)
                for c in range(NC):
                    if not (isinstance(i, int) and i == 0) and c == 0:
                        act.wait_ge(s_qhl, i * 2)
                    act.activation(xTf[:, c], M1[:, c], ident_f, bias=cur[:, par, 2 + c:3 + c],
                                   scale=cur[:, par, c:c + 1]).then_inc(s_xTf, 1)

            def qk_evac(i, c, M):
                act.wait_ge(s_qk, i * 2 + c + 1)
                if c > 0:
                    act.wait_ge(s_qhl, i * 2 + c)
                else:
                    act.wait_ge(s_xhl, i + 1)
                act.activation(qkf[:, 0], M[:, 0], ident_f, bias=bqk[:, c, 0:1], scale=HD ** -0.5).then_inc(s_qkf, 1)
                act.activation(qkf[:, 1], M[:, 1], ident_f, bias=bqk[:, c, 1:2]).then_inc(s_qkf, 1)

            def probs_evac(i, n):
                act.wait_ge(s_T, i * H + n + 1)
                if not (isinstance(i, int) and i == 0 and n < PT_RING):
                    act.wait_ge(s_ctx, i * NG + n // GROUP - 1)
                act.activation(PT[:, n % PT_RING], pT[n % 2][:], ACT.Copy).then_inc(s_ptA, 1)

            def prologue():
                act.wait_ge(s_cst, 1)
                ang = g[:, 4, 0:64]
                act.activation(g[:, 5, 0:64], ang, ACT.Sin).then_inc(s_sin, 1)
                act.wait_ge(s_sin, 1)
                act.activation(g[:, 5, 64:128], g[:, 5, 0:64], ACT.Tanh, scale=0.5).then_inc(s_tanh0, 1)
                x_evac(0, 0)
                qk_evac(0, 0, M1)
                qk_evac(0, 1, M0)

            def body(j, par, att, nxt, post, sten):
                i = j * 2 + par
                b = i - 1
                zero = isinstance(i, int) and i == 0
                first = isinstance(b, int) and b == 0
                for h in range(2 * H):
                    n = h // 2
                    if h % 2 == 0 and att:
                        for t in range(NT):
                            act.wait_ge(s_ttr, i * 32 + 2 * n + t + 1)
                            if t == 0 and (n >= P_RING or not zero):
                                act.wait_ge(s_T, i * H + n - P_RING + 1)
                            act.activation(Pb[:, n % P_RING, t], bias[:, n // GROUP, n % GROUP, t], ACT.Exp, scale=-1.0,
                                           bias=nmax[:, n, t:t + 1],
                                           accum_out=sums[:, par, t, head_of(n):head_of(n) + 1]).then_inc(s_exp, 1)
                    if h % 2 == 1 and n % 2 in PT_ON_ACT:
                        if n >= 2 and att:
                            probs_evac(i, n - 2)
                        if n < 2 and post:
                            probs_evac(b, n - 2 + H)
                    if nxt and h == AT_ACT["x.T"]:
                        x_evac(i + 1, 1 - par)
                    for c in range(NC):
                        if nxt and h == AT_ACT["qk"][c]:
                            qk_evac(i + 1, c, (M1, M0)[c])
                    if post and h == AT_ACT["rec.T"]:
                        act.wait_ge(s_recT, i)
                        act.activation(recT[:], M1[0:H, 0], ACT.Copy).then_inc(s_recTs, 1)
                    if post and h == AT_ACT["rec spread"]:
                        act.wait_ge(s_rT, i)
                        if not first:
                            act.wait_ge(s_hhl, b)
                        act.activation(rTs[:], M1[:], ACT.Copy).then_inc(s_rTs, 1)
                    if post and h == AT_ACT["h.T"]:
                        act.wait_ge(s_hT, i)
                        act.wait_ge(s_cn, i)
                        for c in range(NC):
                            act.activation(hTf[:, c], M0[:, c], ident_f, bias=be2c[:, c:c + 1],
                                           scale=g2c[:, c:c + 1]).then_inc(s_hTf, 1)
                    for f in range(NF // 2):
                        if post and h == AT_ACT["tanh"][f]:
                            act.wait_ge(s_f1, b * 4 + f + 1)
                            if f >= 2 or not first:
                                act.wait_ge(s_g, b * 4 + f - 1)
                            for m in range(2):
                                act.activation(th[:, f % 2, m], (M0, M1)[f % 2][:, m], ACT.Tanh, scale=GELU / 2,
                                               bias=b1s[:, 2 * f + m:2 * f + m + 1]).then_inc(s_tanh, 1)
                    if sten and h == AT_ACT["relu"]:
                        act.wait_ge(s_zf, i - 1)
                        act.activation(zf[:], zf[:], ACT.Relu).then_inc(s_relu, 1)

            run(act, prologue, body)

        @block.vector
        def _(dve):
            steps = [0]

            def link(ins):
                steps[0] += 1
                ins.then_inc(s_lnk, 1)
                dve.wait_ge(s_lnk, steps[0])

            def column(i):
                return slice(i, i + 1) if isinstance(i, int) else bass.ds(i, 1)

            def norm(i, from_, stat, mv, s_stat, s_mv):
                for t in range(NT):
                    dve.bn_stats(stat[:, t], from_[:, t]).then_inc(s_stat, 1)
                by_itself(dve, (s_stat, (i + 1) * 2))
                for t in range(NT):
                    dve.bn_aggr(mv[:, t], stat[:, t]).then_inc(s_mv, 1)

            def apply_norm(into, from_, mv, rs, s_out):
                for t in range(NT):
                    dve.tensor_scalar(into[:, t], from_[:, t], mv[:, t, 0:1], rs[:, t:t + 1],
                                      ALU.subtract, ALU.mult).then_inc(s_out, 1)

            def norm1(i, par):
                dve.wait_ge(ld_src, (i + 1) * 16)
                norm(i, src, stat1, mv1, s_stat1, s_mv1)

            def cur_copy(i, par):
                dve.tensor_copy(cur[:, par].rearrange("p (a o) -> p a o", o=1), emb[:, :, column(i)]).then_inc(s_cur, 1)

            def apply1(i):
                dve.wait_ge(s_rs1, i + 1)
                if not (isinstance(i, int) and i == 0):
                    dve.wait_ge(s_xT, i)
                if not (isinstance(i, int) and i <= 2):
                    dve.wait_ge(s_hT, i - 2)
                apply_norm(xn, src, mv1, rs1, s_xn)

            def x_split(i, par):
                dve.wait_ge(s_xTf, (i + 1) * 2)
                dve.tensor_copy(xT[:, par, 0], xTf[:]).then_inc(s_xhi, 1)
                dve.wait_ge(s_xhi, i + 1)
                dve.tensor_tensor(xT[:, par, 1], xTf[:], xT[:, par, 0].bitcast(F32), ALU.subtract).then_inc(s_xhl, 1)

            def qk_split(i, c):
                dve.wait_ge(s_qkf, i * 4 + 2 * c + 2)
                if c == 1:
                    dve.wait_ge(scat[0], (i + 1) * (16 * 4 * PARTS))
                elif not (isinstance(i, int) and i == 0):
                    dve.wait_ge(scat[1], i * (16 * 4 * PARTS))
                dve.tensor_copy(qk[:, 0], qkf[:]).then_inc(s_qhi, 1)
                dve.wait_ge(s_qhi, i * 2 + c + 1)
                dve.tensor_tensor(qk[:, 1], qkf[:], qk[:, 0].bitcast(F32), ALU.subtract).then_inc(s_qhl, 1)

            def probs_evac(i, n):
                dve.wait_ge(s_T, i * H + n + 1)
                if not (isinstance(i, int) and i == 0 and n < PT_RING):
                    dve.wait_ge(s_ctx, i * NG + n // GROUP - 1)
                dve.tensor_copy(PT[:, n % PT_RING], pT[n % 2][:]).then_inc(s_ptD, 1)

            def prologue():
                dve.wait_ge(ld_c, 16 * 13)
                ti = th[:, 0, 0, 0:B]
                tf, kk, tmp = g[:, 6, 0:32], g[:, 6, 64:96], g[:, 6, 96:128]
                ang = g[:, 4, 0:64].rearrange("p (k b) -> p k b", k=2)
                fr = emb[:, 0, 4:5]
                link(dve.tensor_copy(bad[:, 0:4], emb[:, 0, 0:4]))
                link(dve.tensor_copy(tf, ti.bitcast(I32)))
                link(dve.tensor_scalar(tf, tf, 0.01, 4000.0, ALU.mult, ALU.mult))
                link(dve.tensor_scalar(tf, tf, fr, None, ALU.mult))
                magic = 1.5 * 2 ** 23
                link(dve.tensor_scalar(kk, tf, 0.15915494309189535, magic, ALU.mult, ALU.add))
                link(dve.tensor_scalar(kk, kk, magic, None, ALU.subtract))
                two_pi = 6.283185307179586
                c1 = 6.28125
                c2 = round((two_pi - c1) * 2 ** 20) / 2 ** 20
                c3 = two_pi - c1 - c2
                for cc in (c1, c2, c3):
                    link(dve.scalar_tensor_tensor(out=tf, in0=kk, scalar=-cc, in1=tf, op0=ALU.mult, op1=ALU.add))
                pi = 3.1415925
                link(dve.tensor_scalar(ang[:, 0, :], tf, pi, -pi, ALU.min, ALU.max))
                link(dve.tensor_scalar(tf, tf, two_pi / 4, None, ALU.add))
                link(dve.tensor_scalar(tmp, tf, two_pi / 2, -two_pi, ALU.is_gt, ALU.mult))
                link(dve.tensor_tensor(tf, tf, tmp, ALU.add))
                dve.tensor_scalar(ang[:, 1, :], tf, pi, -pi, ALU.min, ALU.max).then_inc(s_cst, 1)
                norm1(0, 0)
                dve.wait_ge(s_tanh0, 1)
                sn, ta = g[:, 5, 0:64], g[:, 5, 64:128]
                link(dve.scalar_tensor_tensor(out=ta, in0=ta, scalar=1.0, in1=sn, op0=ALU.add, op1=ALU.mult))
                dve.tensor_scalar(g[:, 4, 64:128], ta, 0.5, None, ALU.mult).then_inc(s_emb, 1)
                apply1(0)
                dve.wait_ge(s_embmm, 1)
                for m in range(4):
                    link(dve.tensor_scalar(emb[:, m, :], M2[:, 0, m * B:(m + 1) * B], bad[:, m:m + 1],
                                           1.0 if m < 2 else 0.0, ALU.add, ALU.add))
                cur_copy(0, 0)
                link(dve.tensor_scalar(bqk[:, :, 0], bqk[:, :, 0], HD ** -0.5, None, ALU.mult))
                link(dve.tensor_scalar(b1s[:], b1c[:], GELU / 2, None, ALU.mult))
                dve.wait_ge(s_id, 3)
                link(dve.tensor_copy(ident_b[:], ident[:]))
                dve.tensor_copy(ident_r[:], ident[:]).then_inc(s_split, 1)
                ring = PT[:].rearrange("p a t s -> p (a t s)")

                def split_weight(k, hl, raw):
                    dve.wait_ge(ld_w[k], 16)
                    link(dve.tensor_copy(hl[:, 0], raw))
                    return dve.tensor_tensor(hl[:, 1], raw, hl[:, 0].bitcast(F32), ALU.subtract)

                raws = [ring[:, k * NC * D:(k + 1) * NC * D].rearrange("p (k n) -> p k n", k=NC) for k in range(4)]
                split_weight(0, wq_hl, raws[0])
                x_split(0, 0)
                split_weight(1, wk_hl, raws[1]).then_inc(s_split, 1)
                split_weight(2, wv_hl, raws[2]).then_inc(s_split, 1)
                qk_split(0, 0)
                qk_split(0, 1)
                split_weight(3, wo_hl, raws[3]).then_inc(s_split, 1)
                split_weight(4, w1_hl, ring[:, 2048:4096].rearrange("p (k n) -> p k n", k=NC)).then_inc(s_split, 1)
                dve.wait_ge(ld_g, 16 * 6)
                for end in range(2):
                    sg = 1.0 if end == 0 else -1.0
                    for k, (cb, ca, c2_) in enumerate(((1.0, 1.5, -3.0), (-2.5, -2.0, 4.0), (2.0, 0.5, -1.0), (-0.5, 0.0, 0.0))):
                        o, k = (k, k) if end == 0 else (S - 1 - k, 3 - k)
                        link(dve.tensor_scalar(edge[:, :, end, k:k + 1], gR[:, :, o:o + 1], sg * ca, None, ALU.mult))
                        link(dve.scalar_tensor_tensor(out=edge[:, :, end, k:k + 1], in0=gC[:, :, o:o + 1], scalar=cb,
                                                      in1=edge[:, :, end, k:k + 1], op0=ALU.mult, op1=ALU.add))
                        link(dve.tensor_scalar(edge[:, :, 2 + end, k:k + 1], gB2[:, :, o:o + 1], sg * c2_, None, ALU.mult))
                link(dve.tensor_scalar(gA0, gA0, -2.0, None, ALU.mult))
                link(dve.tensor_tensor(gL, gC, gR, ALU.add))
                link(dve.tensor_tensor(gR, gC, gR, ALU.subtract))
                link(dve.tensor_scalar(gL, gL, 0.5, None, ALU.mult))
                link(dve.tensor_scalar(gR, gR, 0.5, None, ALU.mult))
                link(dve.tensor_scalar(gC, gC, -1.0, None, ALU.mult))

            def body(j, par, att, nxt, post, sten):
                i = j * 2 + par
                b = i - 1
                d = i - 2
                zero = isinstance(i, int) and i == 0
                first = isinstance(b, int) and b == 0
                dfirst = isinstance(d, int) and d == 0
                for h in range(2 * H):
                    n = h // 2
                    if h % 2 == 0 and att:
                        by_itself(dve, (s_S, i * H + n + 1), *([(ld_bias[n // GROUP], i * 32 + 32)] if n % GROUP == 0 else []))
                        for t in range(NT):
                            dve.tensor_tensor_reduce(out=bias[:, n // GROUP, n % GROUP, t], in0=pS[n % 2][:, t],
                                                     in1=bias[:, n // GROUP, n % GROUP, t], scale=-1.0, scalar=HUGE,
                                                     op0=ALU.add, op1=ALU.min,
                                                     accum_out=nmax[:, n, t:t + 1]).then_inc(s_ttr, 1)
                    if h % 2 == 1 and n % 2 not in PT_ON_ACT:
                        if n >= 2 and att:
                            probs_evac(i, n - 2)
                        if n < 2 and post:
                            probs_evac(b, n - 2 + H)
                    if nxt and h == AT_DVE["norm1"]:
                        cur_copy(i + 1, 1 - par)
                        norm1(i + 1, 1 - par)
                    if nxt and h == AT_DVE["x"]:
                        apply1(i + 1)
                    if nxt and h == AT_DVE["x split"]:
                        if post:
                            dve.wait_ge(s_wo, i)
                        x_split(i + 1, 1 - par)
                    for c in range(NC):
                        if nxt and h == AT_DVE["qk split"][c]:
                            qk_split(i + 1, c)
                    if att and h == AT_DVE["v"]:
                        dve.wait_ge(s_v, i + 1)
                        if zero:
                            dve.wait_ge(s_zero, 3)
                        if not zero:
                            dve.wait_ge(s_ctx, i * NG)
                        for t in range(NT):
                            for e in range(2):
                                last = dve.tensor_tensor(
                                    V[:, t, e::2, HD * e:HD * e + HD],
                                    M0[:, t, :].rearrange("p (h e d) -> p h e d", e=2, d=HD)[:, :, e, :],
                                    bv_row[:].rearrange("p (h e d) -> p h e d", e=2, d=HD)[:, :, e, :], ALU.add)
                        last.then_inc(s_vev, 1)
                    if post and h == AT_DVE["rec"]:
                        dve.wait_ge(s_exp, i * 32)
                        if not first:
                            dve.wait_ge(s_recT, b)
                        dve.reciprocal(rec[:], sums[:, 1 - par]).then_inc(s_rec, 1)
                    if post and h == AT_DVE["context"]:
                        dve.wait_ge(s_ctx, i * NG)
                        dve.wait_ge(s_rTs, i)
                        if not first:
                            dve.wait_ge(s_x2b, b * 2)
                        dve.tensor_tensor(cn[:], pC_[:], rTs[:], ALU.mult).then_inc(s_cn, 1)
                        dve.wait_ge(s_cn, i)
                        dve.tensor_copy(cT[:, 0], cn[:]).then_inc(s_chi, 1)
                        dve.wait_ge(s_chi, i)
                        dve.tensor_tensor(cT[:, 1], cn[:], cT[:, 0].bitcast(F32), ALU.subtract).then_inc(s_chl, 1)
                    if post and h == AT_DVE["x2"]:
                        dve.wait_ge(s_wo, i)
                        for t in range(NT):
                            dve.tensor_tensor(x2[:, t], M0[:, t], bo_row[:], ALU.add).then_inc(s_x2, 1)
                        dve.wait_ge(s_x2, i * 2)
                        norm(b, x2, stat2, mv2, s_stat2, s_mv2)
                    if post and h == AT_DVE["h"]:
                        dve.wait_ge(s_rs2, i)
                        if nxt:
                            dve.wait_ge(s_xT, i + 2)
                        apply_norm(hn, x2, mv2, rs2, s_hn)
                    if post and h == AT_DVE["h split"]:
                        dve.wait_ge(s_hTf, i * 2)
                        dve.tensor_copy(hT[:, 0], hTf[:]).then_inc(s_hhi, 1)
                        dve.wait_ge(s_hhi, i)
                        dve.tensor_tensor(hT[:, 1], hTf[:], hT[:, 0].bitcast(F32), ALU.subtract).then_inc(s_hhl, 1)
                    for f in range(NF // 2):
                        if post and h == AT_DVE["gelu"][f]:
                            dve.wait_ge(s_th1, b * 4 + f + 1)
                            if f == 0 and not first:
                                dve.wait_ge(s_f2, b)
                            for m in range(2):
                                last = dve.scalar_tensor_tensor(out=g[:, 2 * f + m], in0=(M0, M1)[f % 2][:, m],
                                                                scalar=b1c[:, 2 * f + m:2 * f + m + 1], in1=th[:, f % 2, m],
                                                                op0=ALU.add, op1=ALU.mult)
                            last.then_inc(s_g, 1)
                    if sten and h == AT_DVE["edges"]:
                        dve.wait_ge(s_x3, d + 1)
                        for end in range(2):
                            f4 = x3[:, :, 0:4] if end == 0 else x3[:, :, S - 4:S]
                            for kind in range(2):
                                dve.tensor_tensor(ed[:, :, 2 * kind + end, :], f4, edge[:, :, 2 * kind + end, :], ALU.mult)\
                                    .then_inc(s_ed, 1)
                    if sten and h == AT_DVE["edge sums"]:
                        dve.wait_ge(s_ed, (d + 1) * 4)
                        dve.tensor_reduce(out=tt[:, :, 0:S:S - 1], in_=ed[:, :, 0:2, :], axis=AXES.X, op=ALU.add).then_inc(s_te, 1)
                        dve.tensor_reduce(out=u1e[:], in_=ed[:, :, 2:4, :], axis=AXES.X, op=ALU.add).then_inc(s_e1, 1)
                        dve.wait_ge(s_e1, d + 1)
                        dve.wait_ge(s_a0f, d + 1)
                        dve.tensor_tensor(u1[:, :, 0:S:S - 1], u1[:, :, 0:S:S - 1], u1e[:], ALU.add).then_inc(s_u1e, 1)
                    if sten and h == AT_DVE["z"]:
                        dve.wait_ge(s_st, d + 1)
                        dve.wait_ge(s_tt, (d + 1) * 2)
                        dve.wait_ge(s_te, d + 1)
                        dve.tensor_tensor(yy[:], M2[:], tt[:], ALU.add).then_inc(s_y, 1)
                        dve.wait_ge(s_y, d + 1)
                        dve.wait_ge(s_dcur, d + 1)
                        dve.scalar_tensor_tensor(out=zf[:], in0=yy[:], scalar=dcur[:, 0:1], in1=x3[:],
                                                 op0=ALU.mult, op1=ALU.add).then_inc(s_zf, 1)
                    if post and h == AT_DVE["x3"]:
                        dve.wait_ge(s_f2, i)
                        dve.wait_ge(s_x2b, i * 2)
                        if not first:
                            dve.wait_ge(s_zf, b)
                        dve.tensor_copy(dcur[:], dt_row[:, column(b)]).then_inc(s_dcur, 1)
                        dve.scalar_tensor_tensor(out=x3[:], in0=M2[:], scalar=0.5, in1=x2b[:],
                                                 op0=ALU.mult, op1=ALU.add).then_inc(s_x3, 1)

            run(dve, prologue, body)


def _stencil_matrices(np):
    m = np.zeros((2, S, S), np.float32)
    for k in range(1, S - 1):
        m[0, k + 1, k], m[0, k - 1, k] = 0.25, -0.25
        m[1, k + 1, k], m[1, k, k], m[1, k - 1, k] = 0.5, -1.0, 0.5
    m[0, 0:3, 0] = (-0.75, 1.0, -0.25)
    m[0, S - 3:, S - 1] = (0.25, -1.0, 0.75)
    m[1, 0:4, 0] = (1.0, -2.5, 2.0, -0.5)
    m[1, S - 4:, S - 1] = (-0.5, 2.0, -2.5, 1.0)
    return m


def kernel(**inputs):
    import numpy as np
    import concourse.bacc as bacc
    from concourse.bass_utils import run_bass_kernel_spmd

    def stacked(w):
        w = np.asarray(w)
        return w.reshape(-1, NC, 4, 2, HD).transpose(0, 1, 3, 4, 2).reshape(w.shape)

    given = {k: np.asarray(v) for k, v in inputs.items()}
    layer = lambda name: given["L0_cond_" + name]
    arrays = {
        "x": given["x"], "itok": given["itok_B_34_63"], "fside": given["fside_Bx16xSxS_0"], "dt": given["condB_dt"],
        "mask": given["mask_Bx1xSxS_bk0"].view(np.int32).reshape(B, S, S // 4),
        "W_ada": layer("W_ada"), "b_ada": layer("b_ada"),
        "Wq": stacked(layer("Wq")), "bq": stacked(layer("bq")), "Wk": stacked(layer("Wk")), "bk": stacked(layer("bk")),
        "Wv": layer("Wv"), "bv": layer("bv"), "Wo": layer("Wo"), "bo": layer("bo"),
        "W1": layer("W1"), "b1": layer("b1"), "W2": layer("W2"), "b2": layer("b2"),
        "g2": layer("g2"), "beta2": layer("beta2"),
        "A_grid": given["L1_cond_A_grid"], "B_grid": given["L1_cond_B_grid"],
        "freqs": np.exp(np.arange(P, dtype=np.float32) * np.float32(-np.log(10000.0) / (P - 1))),
        "stencils": _stencil_matrices(np),
        "selector": np.repeat(np.eye(H, dtype=np.float32), HD, axis=1).reshape(H, NC, P),
    }
    nc = bacc.Bacc("TRN2", target_bir_lowering=False, num_devices=1)
    args = []
    for name, a in arrays.items():
        arrays[name] = a = np.ascontiguousarray(a)
        args.append(nc.dram_tensor(name, a.shape, mybir.dt.from_np(a.dtype), kind="ExternalInput").ap())
    out = nc.dram_tensor("out", (B, S, D), F32, kind="ExternalOutput").ap()
    order = ["x", "itok", "fside", "dt", "mask", "W_ada", "b_ada", "Wq", "bq", "Wk", "bk", "Wv", "bv", "Wo", "bo",
             "W1", "b1", "W2", "b2", "g2", "beta2", "A_grid", "B_grid", "freqs", "stencils", "selector"]
    named = dict(zip(arrays, args))
    build(nc, *[named[n] for n in order], out)
    result = run_bass_kernel_spmd(nc, [arrays], core_ids=[0])
    return result.results[0]["out"]
```

```python
import concourse.bass as bass
from concourse import mybir
from contextlib import ExitStack

ALU = mybir.AluOpType
ACT = mybir.ActivationFunctionType
AXES = mybir.AxisListType
F32 = mybir.dt.float32
F32R = mybir.dt.float32r
BF16 = mybir.dt.bfloat16
I32 = mybir.dt.int32
U8 = mybir.dt.uint8

B, S, D, H, HD, FF = 32, 256, 256, 16, 16, 1024
P = 128
NT = S // P
NC = D // P
NF = FF // P
GROUP = 4
NG = H // GROUP
ROWS = 64
PARTS = 3
P_RING, PT_RING = 4, 8
EPS = 1e-5
NEG = -2.0 ** 127
HUGE = 3.4e38
GELU = 1.702


AT_SP = {"src": 15, "mask": 4, "scatter": [7, 29], "bias": [7, 21, 0, 3], "store": 8}
AT_POOL = {"power1": 0, "mask": 21, "power2": 15, "x2b": 29, "one_plus_tanh": [20, 21, 26, 27],
           "g low": [25, 25, 31, 31], "u low": 11,
           "products": 8, "u1": 10, "u2": 0, "sides": 19, "side_sum": 19, "centre_sum": 19}
AT_PE = {"x.T": 8, "qk": [17, 28], "v": 7, "rec.T": 2, "rec spread": 4, "wo": 10,
         "h.T": 16, "ffn1": [20, 20, 22, 24], "ffn2": [27, 31, 32, 32], "stencil": 15}
AT_ACT = {"x.T": 6, "qk": [16, 27], "rec.T": 1, "rec spread": 1, "h.T": 15,
          "tanh": [16, 19, 22, 23], "relu": 27}
AT_DVE = {"norm1": 1, "x": 3, "x split": 15, "qk split": [18, 30], "v": 6, "rec": 0,
          "context": 5, "x2": 12, "h": 14, "h split": 17, "gelu": [21, 22, 25, 27],
          "gelu high": [21, 23, 26, 27], "u high": 9,
          "edges": 4, "edge sums": 7, "z": 24, "x3": 33}
PT_ON_ACT = [0, 1, 2, 4, 5, 8, 9, 10, 11, 13, 14]


def head_of(n):
    c, e, j = n // 8, (n // 4) % 2, n % 4
    return 8 * c + 2 * j + e


def build(nc, x, itok, fside, dt, mask, W_ada, b_ada, Wq, bq, Wk, bk, Wv, bv, Wo, bo, W1, b1, W2, b2,
          g2, beta2, A_grid, B_grid, freqs, stencils, selector, out):
    ctx = ExitStack()
    with ctx:
        def sb(name, shape, dtype=F32):
            return ctx.enter_context(nc.sbuf_tensor(name, shape, dtype))

        def sem(name):
            return ctx.enter_context(nc.semaphore(name))

        ident = sb("ident", [P, P])
        ident_r = sb("ident_r", [P, P], F32R)
        ident_b = sb("ident_b", [P, P], BF16)
        wq_hl = sb("wq_hl", [P, 2, NC, D], F32R)
        wk_hl = sb("wk_hl", [P, 2, NC, D], F32R)
        wv_hl = sb("wv_hl", [P, 2, NC, D], F32R)
        wo_hl = sb("wo_hl", [P, 2, NC, D], F32R)
        w1_hl = sb("w1_hl", [P, 2, NC, FF], F32R)
        w2_hl = sb("w2_hl", [P, 2, NF, D], F32R)
        sten_w = sb("sten_w", [P, 2, NT, S], F32R)
        bqk = sb("bqk", [P, NC, 2])
        b1c = sb("b1c", [P, NF])
        b1s = sb("b1s", [P, NF])
        g2c = sb("g2c", [P, NC])
        be2c = sb("be2c", [P, NC])
        bv_row = sb("bv_row", [P, D])
        bo_row = sb("bo_row", [P, D])
        b2_row = sb("b2_row", [P, D])
        half = sb("half", [P, NT])
        emb = sb("emb", [P, 4, B])
        dt_row = sb("dt_row", [P, B])
        grids = sb("grids", [P, 6, NT, D])
        gA0, gB0, gR, gL, gC, gB2 = (grids[:, k] for k in range(6))
        edge = sb("edge", [P, NT, 4, 4])

        bias = sb("bias", [P, 2, GROUP, NT, S])
        scratch = bias[:, 1].rearrange("p h t s -> p (h t) s")
        mask_w = sb("mask_w", [P, NT, S // 4], I32)
        mneg = sb("mneg", [P, 2, NT, S], BF16)
        src = sb("src", [P, NT, D])
        xn = sb("xn", [P, NT, D])
        xTf = sb("xTf", [P, NC, S])
        xT = sb("xT", [P, 2, 2, NC, S], F32R)
        cur = sb("cur", [P, 2, 4])
        dcur = sb("dcur", [P, 1])
        bad = sb("bad", [P, 4])
        qkf = xTf
        qk = sb("qk", [P, 2, 2, S], F32R)
        Qs = sb("Qs", [P, H // 2, S], F32R)
        Ks = sb("Ks", [P, H, S], F32R)
        V = sb("V", [P, NT, H, 32])
        nmax = sb("nmax", [P, H, NT])
        Pb = sb("Pb", [P, P_RING, NT, S])
        PT = sb("PT", [P, PT_RING, NT, S])
        sums = sb("sums", [P, 2, NT, H])
        recf = sb("recf", [P, NT, H])
        rec = sb("rec", [P, NT, 2, H], F32R)
        recT = sb("recT", [2 * H, S], F32R)
        sel = sb("sel", [2 * H, NC, P], F32R)
        cT = sb("cT", [P, 2, NC, S], F32R)
        stat1 = sb("stat1", [P, NT, 6])
        mv1 = sb("mv1", [P, NT, 2])
        ve1 = sb("ve1", [P, NT])
        rs1 = sb("rs1", [P, NT])
        stat2 = sb("stat2", [P, NT, 6])
        mv2 = sb("mv2", [P, NT, 2])
        ve2 = sb("ve2", [P, NT])
        rs2 = sb("rs2", [P, NT])
        x2 = sb("x2", [P, NT, D])
        cn = x2
        x2b = sb("x2b", [P, NT, D])
        hn = xn
        hTf = sb("hTf", [P, NC, S])
        rTs = hTf
        hT = sb("hT", [P, 2, NC, S], F32R)
        th = sb("th", [P, 2, 2, S])
        g_hl = sb("g_hl", [P, 2, NF, S], F32R)
        x3 = sb("x3", [P, NT, D])
        u1 = sb("u1", [P, NT, D])
        u2 = sb("u2", [P, NT, D])
        u2_hl = sb("u2_hl", [P, 2, NT, D], F32R)
        u1_hl = hT
        pR = a0f = pC = u1
        pL = zf = u2
        tt = sb("tt", [P, NT, D])
        b2f = x2b
        u1e = sb("u1e", [P, NT, 2])
        ed = sb("ed", [P, NT, 4, 4])
        yy = tt

        w2_raw = (x3, tt, u1, u2)
        sten_raw = (x2, x2b)

        def bank(name, shape):
            return ctx.enter_context(nc.psum_tensor(name, shape, F32))

        pS = [bank(f"pS{k}", [P, NT, S]) for k in range(2)]
        pT = [bank(f"pT{k}", [P, NT, S]) for k in range(2)]
        pC_ = bank("pCtx", [P, NC, S])
        M0 = bank("M0", [P, 2, S])
        M1 = bank("M1", [P, 2, S])
        M2 = bank("M2", [P, NT, D])

        ld_w = [sem(f"ld_w{k}") for k in range(6)]
        ld_e = sem("ld_e")
        ld_c = sem("ld_c")
        ld_g = sem("ld_g")
        ld_w2 = sem("ld_W2")
        ld_src = sem("ld_src")
        ld_mask = sem("ld_mask")
        ld_bias = [sem(f"ld_bias{k}") for k in range(NG)]
        scat = [sem(f"scat{c}") for c in range(NC)]
        stored = sem("stored")
        s_id = sem("s_id")
        s_cst = sem("s_cst")
        s_emb = sem("s_emb")
        s_sin = sem("s_sin")
        s_embmm = sem("s_embmm")
        s_tanh0 = sem("s_tanh0")
        s_split = sem("s_split")
        s_stat1 = sem("s_stat1"); s_mv1 = sem("s_mv1"); s_ve1 = sem("s_ve1"); s_rs1 = sem("s_rs1")
        s_stat2 = sem("s_stat2"); s_mv2 = sem("s_mv2"); s_ve2 = sem("s_ve2"); s_rs2 = sem("s_rs2")
        s_cur = sem("s_cur"); s_dcur = sem("s_dcur"); s_lnk = sem("s_lnk")
        s_xn = sem("s_xn"); s_xT = sem("s_xT"); s_xTf = sem("s_xTf"); s_xhi = sem("s_xhi"); s_xhl = sem("s_xhl")
        s_qk = sem("s_qk"); s_qkf = sem("s_qkf"); s_qhi = sem("s_qhi"); s_qhl = sem("s_qhl")
        s_zero = sem("s_zero")
        s_v = sem("s_v"); s_vev = sem("s_vev")
        s_mneg = sem("s_mneg")
        s_S = sem("s_S"); s_ttr = sem("s_ttr"); s_exp = sem("s_exp")
        s_T = sem("s_T"); s_ptA = sem("s_ptA"); s_ptD = sem("s_ptD"); s_ctx = sem("s_ctx")
        s_recf = sem("s_recf"); s_rhi = sem("s_rhi"); s_rec = sem("s_rec"); s_recT = sem("s_recT"); s_recTs = sem("s_recTs"); s_rT = sem("s_rT"); s_rTs = sem("s_rTs")
        s_cn = sem("s_cn"); s_chi = sem("s_chi"); s_chl = sem("s_chl")
        s_wo = sem("s_wo"); s_x2 = sem("s_x2"); s_x2b = sem("s_x2b"); s_hn = sem("s_hn")
        s_hT = sem("s_hT"); s_hTf = sem("s_hTf"); s_hhi = sem("s_hhi"); s_hhl = sem("s_hhl")
        s_f1 = sem("s_f1"); s_tanh = sem("s_tanh"); s_th1 = sem("s_th1"); s_gf = sem("s_gf"); s_ghi = sem("s_ghi"); s_g = sem("s_g")
        s_f2 = sem("s_f2"); s_x3 = sem("s_x3")
        s_b2f = sem("s_b2f"); s_a0f = sem("s_a0f"); s_u2 = sem("s_u2")
        s_pRL = sem("s_pRL"); s_tt = sem("s_tt"); s_pC = sem("s_pC"); s_ed = sem("s_ed")
        s_d1 = sem("s_d1"); s_u1 = sem("s_u1"); s_e1 = sem("s_e1"); s_u1e = sem("s_u1e"); s_uhi = sem("s_uhi"); s_ulo = sem("s_ulo"); s_w2 = sem("s_w2"); s_te = sem("s_te")
        s_st = sem("s_st"); s_y = sem("s_y"); s_zf = sem("s_zf"); s_relu = sem("s_relu")

        FULL = dict(att=True, nxt=True, post=True, sten=True)

        def run(eng, prologue, body):
            prologue()
            body(0, 0, att=True, nxt=True, post=False, sten=False)
            body(0, 1, att=True, nxt=True, post=True, sten=False)
            with eng.Fori(1, B // 2 - 1) as j:
                body(j, 0, **FULL)
                body(j, 1, **FULL)
            body(B // 2 - 1, 0, **FULL)
            body(B // 2 - 1, 1, att=True, nxt=False, post=True, sten=True)
            body(B // 2, 0, att=False, nxt=False, post=True, sten=True)
            body(B // 2, 1, att=False, nxt=False, post=False, sten=True)

        def now(at, h, post, sten, i):
            if at == h and post:
                return i - 1
            return i - 2 if at == h + 2 * H and sten else None

        def evacuated(on_act, i, n):
            if n < 0:
                i, n = i - 1, n + H
            of_act = [m for m in range(H) if m in PT_ON_ACT]
            of_dve = [m for m in range(H) if m not in PT_ON_ACT]
            sem_, of = (s_ptA, of_act) if on_act else (s_ptD, of_dve)
            return sem_, i * len(of) + sum(m <= n for m in of)

        def by_itself(eng, *waits):
            for _, v in waits:
                eng.compute_val(v)
            eng.wait_ge(s_id, 3)
            for s_, v in waits:
                eng.wait_ge(s_, v)

        block = ctx.enter_context(nc.Block())

        @block.sync
        def _(sp):
            def tok(ap):
                return ap.rearrange("(t p) n -> p t n", p=P)

            def at(ap, i):
                return ap[i] if isinstance(i, int) else ap[bass.ds(i, 1)].rearrange("o a n -> (o a) n")

            def load_src(i):
                sp.dma_start(src[:], tok(at(x, i))).then_inc(ld_src, 16)

            def load_mask(i):
                sp.dma_start(mask_w[:], tok(at(mask, i))).then_inc(ld_mask, 16)

            def load_bias(i, n):
                c, e = n // 2, n % 2
                for t in range(NT):
                    rows = (fside[i] if isinstance(i, int) else
                            fside[bass.ds(i, 1)].rearrange("o h q k -> (o h) q k"))
                    part = rows[8 * c + e:8 * c + 8:2, t * P:(t + 1) * P, :].rearrange("h p k -> p h k")
                    sp.dma_start(bias[:, n % 2, :, t, :], part).then_inc(ld_bias[n], 16)

            def scatter(c):
                for s in range(2):
                    for r in range(PARTS):
                        for w, high_low in ((0, (0, 1, 0)), (1, (0, 0, 1))):
                            rows = slice(ROWS * s + HD * r, ROWS * s + HD * (r + 1))
                            into = Qs[rows, 4 * c:4 * c + 4, :] if w == 0 else Ks[rows, 8 * c + s:8 * c + 8:2, :]
                            sp.dma_start(into.bitcast(F32), qk[64 * s:64 * s + 64, high_low[r], w, :].bitcast(F32))\
                              .then_inc(scat[c], 16)

            def prologue():
                ring = PT[:].rearrange("p a t s -> p (a t s)")
                weights = [(w, ring[:, k * NC * D:(k + 1) * NC * D].rearrange("p (k n) -> p k n", k=NC))
                           for k, w in enumerate((Wq, Wk, Wv, Wo))]
                weights.append((W1, ring[:, 2048:4096].rearrange("p (k n) -> p k n", k=NC)))
                weights.append((W_ada, scratch[:, 0:4, :].rearrange("p a b -> p (a b)").rearrange("p (k n) -> p k n", k=2)))

                def load_weight(k):
                    w, into = weights[k]
                    sp.dma_start(into, w.rearrange("(k p) n -> p k n", p=P)).then_inc(ld_w[k], 16)

                sp.dma_start(th[:, 0, 0, 0:B].bitcast(I32), itok.partition_broadcast(P)).then_inc(ld_e, 16)
                with nc.allow_non_contiguous_dma(reason="small vectors, once"):
                    sp.dma_start(emb[:, 0, 4:5], freqs.rearrange("(p o) -> p o", o=1)).then_inc(ld_e, 16)
                    load_src(0)
                    load_weight(5)
                    load_weight(0)
                    for from_, into in ((b_ada.rearrange("(m p) -> p m", p=P), bad[:]),
                                        (bq.rearrange("(c p) -> p c", p=P), bqk[:, :, 0]),
                                        (bk.rearrange("(c p) -> p c", p=P), bqk[:, :, 1])):
                        sp.dma_start(into, from_).then_inc(ld_c, 16)
                    load_weight(1)
                    for from_, into in ((b1.rearrange("(m p) -> p m", p=P), b1c[:]),
                                        (g2.rearrange("(c p) -> p c", p=P), g2c[:]),
                                        (beta2.rearrange("(c p) -> p c", p=P), be2c[:])):
                        sp.dma_start(into, from_).then_inc(ld_c, 16)
                load_mask(0)
                load_weight(2)
                for from_, into in ((bv, bv_row), (bo, bo_row), (b2, b2_row), (dt, dt_row)):
                    sp.dma_start(into[:], from_.partition_broadcast(P)).then_inc(ld_c, 16)
                sp.dma_start(scratch[0:2 * H, 7], selector.rearrange("h c p -> h (c p)")).then_inc(ld_c, 16)
                load_bias(0, 0)
                load_weight(3)
                load_weight(4)
                sp.wait_ge(s_cur, 1)
                load_bias(0, 1)
                for q, into in enumerate(w2_raw):
                    sp.dma_start(into[:], W2[2 * q * P:2 * (q + 1) * P].rearrange("(k p) n -> p k n", p=P)).then_inc(ld_w2, 16)
                for g_, into in ((A_grid[0], gA0), (B_grid[0], gB0), (A_grid[1], gR), (B_grid[1], gC), (B_grid[2], gB2)):
                    sp.dma_start(into, tok(g_)).then_inc(ld_g, 16)
                for m, into in enumerate(sten_raw):
                    sp.dma_start(into[:], stencils[m].rearrange("(k p) n -> p k n", p=P)).then_inc(ld_g, 16)
                sp.wait_ge(s_xn, 2)
                load_src(1)
                for c in range(NC):
                    if c == 0:
                        sp.wait_ge(s_zero, 2)
                    sp.wait_ge(s_qhl, c + 1)
                    scatter(c)

            def body(j, par, att, nxt, post, sten):
                i = j * 2 + par
                for h in range(2 * H):
                    if nxt and h == AT_SP["src"] and not (isinstance(i, int) and i + 2 >= B):
                        by_itself(sp, (s_xn, (i + 2) * 2))
                        load_src(i + 2)
                    if nxt and h == AT_SP["mask"]:
                        by_itself(sp, (s_mneg, i + 1))
                        load_mask(i + 1)
                    for c in range(NC):
                        if nxt and h == AT_SP["scatter"][c]:
                            by_itself(sp, (s_qhl, (i + 1) * 2 + c + 1), (s_S, i * H + 8 * c + 8))
                            scatter(c)
                    for gr in range(NG):
                        if gr < 2 and nxt and h == AT_SP["bias"][gr]:
                            by_itself(sp, (s_exp, i * 32 + 8 * gr + 24))
                            load_bias(i + 1, gr)
                        if gr >= 2 and att and h == AT_SP["bias"][gr]:
                            by_itself(sp, (s_exp, i * 32 + 8 * gr - 8))
                            load_bias(i, gr)
                    if sten and h == AT_SP["store"]:
                        by_itself(sp, (s_relu, i - 1))
                        sp.dma_start(tok(at(out, i - 2)), zf[:]).then_inc(stored, 16)

            run(sp, prologue, body)
            sp.wait_ge(stored, 16 * B)

        @block.gpsimd
        def _(pool):
            def mask_values(i, par):
                waits = [(ld_mask, i * 16 + 16)]
                if not (isinstance(i, int) and i < 2):
                    waits.append((s_S, (i - 1) * H))
                by_itself(pool, *waits)
                pool.tensor_scalar(mneg[:, par], mask_w[:].bitcast(U8), NEG, 1.0, ALU.mult, ALU.mult).then_inc(s_mneg, 1)

            def power(mv, ve, rs, s_mv, s_ve, s_rs, i):
                by_itself(pool, (s_mv, (i + 1) * 2))
                pool.tensor_scalar(ve[:], mv[:, :, 1], EPS, 1.0, ALU.add, ALU.mult).then_inc(s_ve, 1)
                pool.wait_ge(s_ve, i + 1)
                pool.tensor_tensor(rs[:], ve[:], half[:], ALU.pow).then_inc(s_rs, 1)

            def prologue():
                pool.memset(ident[:], 0.0).then_inc(s_id, 1)
                pool.memset(half[:], -0.5).then_inc(s_id, 1)
                pool.wait_ge(s_id, 2)
                pool.affine_select(out=ident[:], in_=ident[:], compare_op=ALU.not_equal, fill=1.0, base=0,
                                   pattern=[[-1, P]], channel_multiplier=1).then_inc(s_id, 1)
                power(mv1, ve1, rs1, s_mv1, s_ve1, s_rs1, 0)
                pool.memset(Ks[:].bitcast(F32), 0.0).then_inc(s_zero, 1)
                pool.memset(Qs[:].bitcast(F32), 0.0).then_inc(s_zero, 1)
                pool.memset(V[:], 0.0).then_inc(s_zero, 1)
                mask_values(0, 0)

            def body(j, par, att, nxt, post, sten):
                i = j * 2 + par
                b, d = i - 1, i - 2
                first = isinstance(b, int) and b == 0
                dfirst = isinstance(d, int) and d == 0
                u_in, t_in = u1[:, :, 1:S - 1], tt[:, :, 1:S - 1]
                for h in range(2 * H):
                    if nxt and h == AT_POOL["power1"]:
                        power(mv1, ve1, rs1, s_mv1, s_ve1, s_rs1, i + 1)
                    if nxt and h == AT_POOL["mask"]:
                        mask_values(i + 1, 1 - par)
                    if post and h == AT_POOL["power2"]:
                        power(mv2, ve2, rs2, s_mv2, s_ve2, s_rs2, b)
                    if post and h == AT_POOL["x2b"]:
                        pool.wait_ge(s_x2, i * 2)
                        if not first:
                            pool.wait_ge(s_x3, b)
                        if sten:
                            pool.wait_ge(s_u1, d + 1)
                        for t in range(NT):
                            pool.tensor_tensor(x2b[:, t], x2[:, t], b2_row[:], ALU.add).then_inc(s_x2b, 1)
                    for f in range(NF // 2):
                        if post and h == AT_POOL["one_plus_tanh"][f]:
                            by_itself(pool, (s_tanh, b * 8 + 2 * f + 2))
                            pool.tensor_scalar(th[:, f % 2], th[:, f % 2], 1.0, 1.0, ALU.add, ALU.mult).then_inc(s_th1, 1)
                        if post and h == AT_POOL["g low"][f]:
                            pool.wait_ge(s_ghi, b * 4 + f + 1)
                            pool.tensor_tensor(g_hl[:, 1, 2 * f:2 * f + 2], th[:, f % 2],
                                               g_hl[:, 0, 2 * f:2 * f + 2].bitcast(F32), ALU.subtract).then_inc(s_g, 1)
                    if sten and h == AT_POOL["products"]:
                        pool.wait_ge(s_x3, d + 1)
                        if not dfirst:
                            pool.wait_ge(s_tt, d * 2)
                        pool.tensor_tensor(a0f[:], x3[:], gA0, ALU.mult).then_inc(s_a0f, 1)
                        pool.tensor_tensor(b2f[:], x3[:], gB2, ALU.mult).then_inc(s_b2f, 1)
                    if sten and h == AT_POOL["u1"]:
                        pool.wait_ge(s_a0f, d + 1)
                        pool.wait_ge(s_b2f, d + 1)
                        pool.tensor_tensor(u_in, u_in, b2f[:, :, 2:S], ALU.add).then_inc(s_d1, 1)
                        pool.wait_ge(s_d1, d + 1)
                        pool.tensor_tensor(u_in, u_in, b2f[:, :, 0:S - 2], ALU.subtract).then_inc(s_u1, 1)
                    if sten and h == AT_POOL["u2"]:
                        pool.wait_ge(s_x3, d + 1)
                        if not dfirst:
                            pool.wait_ge(stored, d * 16)
                        pool.tensor_tensor(u2[:], x3[:], gB0, ALU.mult).then_inc(s_u2, 1)
                    if sten and h == AT_POOL["u low"]:
                        pool.wait_ge(s_uhi, (d + 1) * 2)
                        for u, hl in ((u1, u1_hl), (u2, u2_hl)):
                            pool.tensor_tensor(hl[:, 1], u[:], hl[:, 0].bitcast(F32), ALU.subtract).then_inc(s_ulo, 1)
                    if sten and h == AT_POOL["sides"]:
                        pool.wait_ge(s_ulo, (d + 1) * 2)
                        pool.tensor_tensor(pR[:], x3[:], gR, ALU.mult).then_inc(s_pRL, 1)
                        pool.tensor_tensor(pL[:], x3[:], gL, ALU.mult).then_inc(s_pRL, 1)
                    if sten and h == AT_POOL["side_sum"]:
                        pool.wait_ge(s_pRL, (d + 1) * 2)
                        if not dfirst:
                            pool.wait_ge(s_zf, d)
                        pool.tensor_tensor(t_in, pR[:, :, 2:S], pL[:, :, 0:S - 2], ALU.add).then_inc(s_tt, 1)
                        pool.wait_ge(s_tt, d * 2 + 1)
                        pool.tensor_tensor(pC[:], x3[:], gC, ALU.mult).then_inc(s_pC, 1)
                    if sten and h == AT_POOL["centre_sum"]:
                        pool.wait_ge(s_pC, d + 1)
                        pool.tensor_tensor(t_in, t_in, pC[:, :, 1:S - 1], ALU.add).then_inc(s_tt, 1)

            run(pool, prologue, body)

        @block.tensor
        def _(pe):
            mm = nc.tensor.matmul

            def split_mm(into, lhs, rhs, k, nk, close=True):
                for m, (a, b) in enumerate(((0, 0), (1, 0), (0, 1))):
                    last = mm(into, lhs[a], rhs[b], start=(k == 0 and m == 0),
                              stop=(close and k == nk - 1 and m == 2))
                return last

            def transposes(into, from_):
                for c in range(2):
                    for t in range(2):
                        last = nc.tensor.transpose(into[:, c, t * P:(t + 1) * P], from_(t, c), ident[:])
                return last

            def x_transposed(i):
                pe.wait_ge(s_xn, (i + 1) * 2)
                transposes(M1, lambda t, c: xn[:, t, c * P:(c + 1) * P]).then_inc(s_xT, 1)

            def qk_product(i, par, c, M):
                for w, wt in ((0, wq_hl), (1, wk_hl)):
                    for k in range(NC):
                        last = split_mm(M[:, w, :], [wt[:, a, k, c * P:(c + 1) * P] for a in (0, 1)],
                                        [xT[:, par, a, k, :] for a in (0, 1)], k, NC)
                last.then_inc(s_qk, 1)

            def scores(i, par, n):
                if n % 8 == 0:
                    pe.wait_ge(scat[n // 8], (i + 1) * (16 * 4 * PARTS))
                if n == 0:
                    pe.wait_ge(s_mneg, i + 1)
                if n >= 2 or not (isinstance(i, int) and i == 0):
                    pe.wait_ge(s_ttr, i * 32 + 2 * n - 2)
                hd = head_of(n)
                for t in range(NT):
                    mm(pS[n % 2][:, t, :], Qs[:, hd // 2, t * P:(t + 1) * P], Ks[:, hd, :], start=True, stop=False)
                    last = mm(pS[n % 2][:, t, :], ident_b[:], mneg[:, par, t, :], start=False, stop=True)
                last.then_inc(s_S, 1)

            def transposed_probs(i, n):
                pe.wait_ge(s_exp, i * 32 + 2 * n + 2)
                if n >= 2 or not (isinstance(i, int) and i == 0):
                    pe.wait_ge(*evacuated((n - 2) % H in PT_ON_ACT, i, n - 2))
                for k in range(NT):
                    for t in range(NT):
                        last = nc.tensor.transpose(pT[n % 2][:, k, t * P:(t + 1) * P],
                                                   Pb[:, n % P_RING, t, k * P:(k + 1) * P], ident[:])
                last.then_inc(s_T, 1)

            def context(i, par, gr):
                for on_act in (True, False):
                    sem_, value = evacuated(on_act, i, GROUP * gr + GROUP - 1)
                    if not (isinstance(value, int) and value == 0):
                        pe.wait_ge(sem_, value)
                if gr == 0:
                    pe.wait_ge(s_vev, i + 1)
                    if not (isinstance(i, int) and i == 0):
                        pe.wait_ge(s_cn, i)
                c, e = gr // 2, gr % 2
                for k in range(NT):
                    for q in range(GROUP):
                        n = gr * GROUP + q
                        last = mm(pC_[32 * q:32 * q + 32, c, :], V[:, k, head_of(n), :],
                                  PT[:, n % PT_RING, k, :], start=(e == 0 and k == 0),
                                  stop=(e == 1 and k == NT - 1))
                last.then_inc(s_ctx, 1)

            def prologue():
                pe.wait_ge(s_emb, 1)
                pe.wait_ge(ld_w[5], 16)
                wa = scratch[:, 0:4, :].rearrange("p a b -> p (a b)").rearrange("p (k n) -> p k n", k=2)
                silu = scratch[:, 4, 64:128].rearrange("p (k b) -> p k b", k=2)
                for m in range(4):
                    for k in range(2):
                        last = mm(M2[:, 0, m * B:(m + 1) * B], wa[:, k, m * P:(m + 1) * P], silu[:, k, :],
                                  start=(k == 0), stop=(k == 1))
                last.then_inc(s_embmm, 1)
                pe.wait_ge(s_id, 3)
                x_transposed(0)
                pe.wait_ge(s_split, 2)
                pe.wait_ge(s_xhl, 1)
                qk_product(0, 0, 0, M1)
                qk_product(0, 0, 1, M0)

            def body(j, par, att, nxt, post, sten):
                i = j * 2 + par
                b = i - 1
                zero = isinstance(i, int) and i == 0
                first = isinstance(b, int) and b == 0
                for h in range(2 * H):
                    n = h // 2
                    if h % 2 == 0 and att:
                        scores(i, par, n)
                    if h % 2 == 1:
                        if n >= 2 and att:
                            transposed_probs(i, n - 2)
                        if n < 2 and post:
                            transposed_probs(b, n - 2 + H)
                        gr = n // GROUP - 1
                        if n % GROUP == 2 and gr >= 0 and att:
                            context(i, par, gr)
                        if n % GROUP == 2 and gr < 0 and post:
                            context(b, 1 - par, NG - 1)
                    if nxt and h == AT_PE["x.T"]:
                        if post:
                            pe.wait_ge(s_rTs, i)
                        x_transposed(i + 1)
                    if nxt and h == AT_PE["qk"][0]:
                        pe.wait_ge(s_xhl, i + 2)
                        qk_product(i + 1, 1 - par, 0, M1)
                    if nxt and h == AT_PE["qk"][1]:
                        if post:
                            pe.wait_ge(s_gf, b * 4 + 3)
                        qk_product(i + 1, 1 - par, 1, M0)
                    if att and h == AT_PE["v"]:
                        if zero:
                            pe.wait_ge(s_split, 3)
                        pe.wait_ge(s_qkf, (i + 1) * 4)
                        for t in range(NT):
                            for k in range(NC):
                                last = split_mm(M0[:, t, :], [xT[:, par, a, k, t * P:(t + 1) * P] for a in (0, 1)],
                                                [wv_hl[:, a, k, :] for a in (0, 1)], k, NC)
                        last.then_inc(s_v, 1)
                    if post and h == AT_PE["rec.T"]:
                        if not first:
                            pe.wait_ge(s_gf, b * 4)
                        pe.wait_ge(s_rec, i)
                        for t in range(NT):
                            last = nc.tensor.transpose(M1[0:2 * H, 0, t * P:(t + 1) * P],
                                                       rec[:, t].rearrange("p a h -> p (a h)").bitcast(F32), ident[:])
                        last.then_inc(s_recT, 1)
                    if post and h == AT_PE["rec spread"]:
                        pe.wait_ge(s_recTs, i)
                        for c in range(NC):
                            last = mm(M1[:, c, :], sel[:, c, :], recT[:], start=True, stop=True)
                        last.then_inc(s_rT, 1)
                    if post and h == AT_PE["wo"]:
                        if att:
                            pe.wait_ge(s_vev, i + 1)
                        pe.wait_ge(s_chl, i)
                        for t in range(NT):
                            for k in range(NC):
                                split_mm(M0[:, t, :], [cT[:, a, k, t * P:(t + 1) * P] for a in (0, 1)],
                                         [wo_hl[:, a, k, :] for a in (0, 1)], k, NC, close=False)
                            for c in range(NC):
                                for a in (0, 1):
                                    last = mm(M0[:, t, c * P:(c + 1) * P], xT[:, 1 - par, a, c, t * P:(t + 1) * P],
                                              ident_r[:], start=False, stop=(c == NC - 1 and a == 1))
                        last.then_inc(s_wo, 1)
                    if post and h == AT_PE["h.T"]:
                        pe.wait_ge(s_hn, i * 2)
                        transposes(M0, lambda t, c: hn[:, t, c * P:(c + 1) * P]).then_inc(s_hT, 1)
                    for f in range(NF // 2):
                        if post and h == AT_PE["ffn1"][f]:
                            M = (M0, M1)[f % 2]
                            if f == 0:
                                pe.wait_ge(s_hhl, i)
                            if f == 1 and nxt:
                                pe.wait_ge(s_qkf, (i + 1) * 4 + 2)
                            if f >= 2:
                                pe.wait_ge(s_gf, b * 4 + f - 1)
                            for m in range(2):
                                for k in range(NC):
                                    last = split_mm(M[:, m, :],
                                                    [w1_hl[:, a, k, (2 * f + m) * P:(2 * f + m + 1) * P] for a in (0, 1)],
                                                    [hT[:, a, k, :] for a in (0, 1)], k, NC)
                            last.then_inc(s_f1, 1)
                    for q in range(4):
                        m = now(AT_PE["ffn2"][q], h, post, sten, i)
                        if m is not None:
                            t, part = q // 2, q % 2
                            if q == 0 and sten:
                                pe.wait_ge(s_y, i - 1)
                            if q == 0 and first:
                                pe.wait_ge(s_w2, len(w2_raw))
                            pe.wait_ge(s_g, m * 4 + 2 * part + 2)
                            for f in range(4 * part, 4 * part + 4):
                                last = split_mm(M2[:, t, :], [g_hl[:, a, f, t * P:(t + 1) * P] for a in (0, 1)],
                                                [w2_hl[:, a, f, :] for a in (0, 1)], f, NF)
                            if q == 3:
                                last.then_inc(s_f2, 1)
                    if sten and h == AT_PE["stencil"]:
                        pe.wait_ge(s_ulo, (i - 1) * 2)
                        pe.wait_ge(s_x3, i - 1)
                        for t in range(NT):
                            for m, u in enumerate((u1_hl, u2_hl)):
                                for k in range(NT):
                                    for a in (0, 1):
                                        last = mm(M2[:, t, :], sten_w[:, m, k, t * P:(t + 1) * P], u[:, a, k, :],
                                                  start=(m == k == a == 0), stop=(m == k == a == 1))
                        last.then_inc(s_st, 1)

            run(pe, prologue, body)

        @block.scalar
        def _(act):
            ident_f = ACT.Identity

            def x_evac(i, par):
                act.wait_ge(s_xT, i + 1)
                act.wait_ge(s_cur, i + 1)
                for c in range(NC):
                    if not (isinstance(i, int) and i == 0) and c == 0:
                        act.wait_ge(s_qhl, i * 2)
                    act.activation(xTf[:, c], M1[:, c], ident_f, bias=cur[:, par, 2 + c:3 + c],
                                   scale=cur[:, par, c:c + 1]).then_inc(s_xTf, 1)

            def qk_evac(i, c, M):
                act.wait_ge(s_qk, i * 2 + c + 1)
                if c > 0:
                    act.wait_ge(s_qhl, i * 2 + c)
                else:
                    act.wait_ge(s_xhl, i + 1)
                act.activation(qkf[:, 0], M[:, 0], ident_f, bias=bqk[:, c, 0:1], scale=HD ** -0.5).then_inc(s_qkf, 1)
                act.activation(qkf[:, 1], M[:, 1], ident_f, bias=bqk[:, c, 1:2]).then_inc(s_qkf, 1)

            def probs_evac(i, n):
                act.wait_ge(s_T, i * H + n + 1)
                if not (isinstance(i, int) and i == 0 and n < PT_RING):
                    act.wait_ge(s_ctx, i * NG + n // GROUP - 1)
                act.activation(PT[:, n % PT_RING], pT[n % 2][:], ACT.Copy).then_inc(s_ptA, 1)

            def prologue():
                act.wait_ge(s_cst, 1)
                ang = scratch[:, 4, 0:64]
                act.activation(scratch[:, 5, 0:64], ang, ACT.Sin).then_inc(s_sin, 1)
                act.wait_ge(s_sin, 1)
                act.activation(scratch[:, 5, 64:128], scratch[:, 5, 0:64], ACT.Tanh, scale=0.5).then_inc(s_tanh0, 1)
                x_evac(0, 0)
                qk_evac(0, 0, M1)
                qk_evac(0, 1, M0)

            def body(j, par, att, nxt, post, sten):
                i = j * 2 + par
                b = i - 1
                zero = isinstance(i, int) and i == 0
                first = isinstance(b, int) and b == 0
                for h in range(2 * H):
                    n = h // 2
                    if h % 2 == 0 and att:
                        for t in range(NT):
                            act.wait_ge(s_ttr, i * 32 + 2 * n + t + 1)
                            if t == 0 and (n >= P_RING or not zero):
                                act.wait_ge(s_T, i * H + n - P_RING + 1)
                            act.activation(Pb[:, n % P_RING, t], bias[:, n // GROUP % 2, n % GROUP, t], ACT.Exp, scale=-1.0,
                                           bias=nmax[:, n, t:t + 1],
                                           accum_out=sums[:, par, t, head_of(n):head_of(n) + 1]).then_inc(s_exp, 1)
                    if h % 2 == 1 and (n - 2) % H in PT_ON_ACT:
                        if n >= 2 and att:
                            probs_evac(i, n - 2)
                        if n < 2 and post:
                            probs_evac(b, n - 2 + H)
                    if nxt and h == AT_ACT["x.T"]:
                        x_evac(i + 1, 1 - par)
                    for c in range(NC):
                        if nxt and h == AT_ACT["qk"][c]:
                            qk_evac(i + 1, c, (M1, M0)[c])
                    if post and h == AT_ACT["rec.T"]:
                        act.wait_ge(s_recT, i)
                        act.activation(recT[:], M1[0:2 * H, 0], ACT.Copy).then_inc(s_recTs, 1)
                    if post and h == AT_ACT["rec spread"]:
                        act.wait_ge(s_rT, i)
                        if not first:
                            act.wait_ge(s_hhl, b)
                        act.activation(rTs[:], M1[:], ACT.Copy).then_inc(s_rTs, 1)
                    if post and h == AT_ACT["h.T"]:
                        act.wait_ge(s_hT, i)
                        act.wait_ge(s_cn, i)
                        for c in range(NC):
                            act.activation(hTf[:, c], M0[:, c], ident_f, bias=be2c[:, c:c + 1],
                                           scale=g2c[:, c:c + 1]).then_inc(s_hTf, 1)
                    for f in range(NF // 2):
                        if post and h == AT_ACT["tanh"][f]:
                            act.wait_ge(s_f1, b * 4 + f + 1)
                            if f >= 2 or not first:
                                act.wait_ge(s_g, b * 4 + f - 1)
                            for m in range(2):
                                act.activation(th[:, f % 2, m], (M0, M1)[f % 2][:, m], ACT.Tanh, scale=GELU / 2,
                                               bias=b1s[:, 2 * f + m:2 * f + m + 1]).then_inc(s_tanh, 1)
                    if sten and h == AT_ACT["relu"]:
                        act.wait_ge(s_zf, i - 1)
                        act.activation(zf[:], zf[:], ACT.Relu).then_inc(s_relu, 1)

            run(act, prologue, body)

        @block.vector
        def _(dve):
            steps = [0]

            def link(ins):
                steps[0] += 1
                ins.then_inc(s_lnk, 1)
                dve.wait_ge(s_lnk, steps[0])

            def column(i):
                return slice(i, i + 1) if isinstance(i, int) else bass.ds(i, 1)

            def norm(i, from_, stat, mv, s_stat, s_mv):
                for t in range(NT):
                    dve.bn_stats(stat[:, t], from_[:, t]).then_inc(s_stat, 1)
                by_itself(dve, (s_stat, (i + 1) * 2))
                for t in range(NT):
                    dve.bn_aggr(mv[:, t], stat[:, t]).then_inc(s_mv, 1)

            def apply_norm(into, from_, mv, rs, s_out):
                for t in range(NT):
                    dve.tensor_scalar(into[:, t], from_[:, t], mv[:, t, 0:1], rs[:, t:t + 1],
                                      ALU.subtract, ALU.mult).then_inc(s_out, 1)

            def norm1(i, par):
                dve.wait_ge(ld_src, (i + 1) * 16)
                norm(i, src, stat1, mv1, s_stat1, s_mv1)

            def cur_copy(i, par):
                dve.tensor_copy(cur[:, par].rearrange("p (a o) -> p a o", o=1), emb[:, :, column(i)]).then_inc(s_cur, 1)

            def apply1(i):
                dve.wait_ge(s_rs1, i + 1)
                if not (isinstance(i, int) and i == 0):
                    dve.wait_ge(s_xT, i)
                if not (isinstance(i, int) and i <= 2):
                    dve.wait_ge(s_hT, i - 2)
                apply_norm(xn, src, mv1, rs1, s_xn)

            def x_split(i, par):
                dve.wait_ge(s_xTf, (i + 1) * 2)
                dve.tensor_copy(xT[:, par, 0], xTf[:]).then_inc(s_xhi, 1)
                dve.wait_ge(s_xhi, i + 1)
                dve.tensor_tensor(xT[:, par, 1], xTf[:], xT[:, par, 0].bitcast(F32), ALU.subtract).then_inc(s_xhl, 1)

            def qk_split(i, c):
                dve.wait_ge(s_qkf, i * 4 + 2 * c + 2)
                if c == 1:
                    dve.wait_ge(scat[0], (i + 1) * (16 * 4 * PARTS))
                elif not (isinstance(i, int) and i == 0):
                    dve.wait_ge(scat[1], i * (16 * 4 * PARTS))
                dve.tensor_copy(qk[:, 0], qkf[:]).then_inc(s_qhi, 1)
                dve.wait_ge(s_qhi, i * 2 + c + 1)
                dve.tensor_tensor(qk[:, 1], qkf[:], qk[:, 0].bitcast(F32), ALU.subtract).then_inc(s_qhl, 1)

            def probs_evac(i, n):
                dve.wait_ge(s_T, i * H + n + 1)
                if not (isinstance(i, int) and i == 0 and n < PT_RING):
                    dve.wait_ge(s_ctx, i * NG + n // GROUP - 1)
                dve.tensor_copy(PT[:, n % PT_RING], pT[n % 2][:]).then_inc(s_ptD, 1)

            def prologue():
                dve.wait_ge(ld_e, 16 * 2)
                ti = th[:, 0, 0, 0:B]
                tf, kk, tmp = scratch[:, 6, 0:32], scratch[:, 6, 64:96], scratch[:, 6, 96:128]
                ang = scratch[:, 4, 0:64].rearrange("p (k b) -> p k b", k=2)
                fr = emb[:, 0, 4:5]
                link(dve.tensor_copy(tf, ti.bitcast(I32)))
                link(dve.tensor_scalar(tf, tf, 0.01, 4000.0, ALU.mult, ALU.mult))
                link(dve.tensor_scalar(tf, tf, fr, None, ALU.mult))
                magic = 1.5 * 2 ** 23
                link(dve.tensor_scalar(kk, tf, 0.15915494309189535, magic, ALU.mult, ALU.add))
                link(dve.tensor_scalar(kk, kk, magic, None, ALU.subtract))
                two_pi = 6.283185307179586
                c1 = 6.28125
                c2 = round((two_pi - c1) * 2 ** 20) / 2 ** 20
                c3 = two_pi - c1 - c2
                for cc in (c1, c2, c3):
                    link(dve.scalar_tensor_tensor(out=tf, in0=kk, scalar=-cc, in1=tf, op0=ALU.mult, op1=ALU.add))
                pi = 3.1415925
                link(dve.tensor_scalar(ang[:, 0, :], tf, pi, -pi, ALU.min, ALU.max))
                link(dve.tensor_scalar(tf, tf, two_pi / 4, None, ALU.add))
                link(dve.tensor_scalar(tmp, tf, two_pi / 2, -two_pi, ALU.is_gt, ALU.mult))
                link(dve.tensor_tensor(tf, tf, tmp, ALU.add))
                dve.tensor_scalar(ang[:, 1, :], tf, pi, -pi, ALU.min, ALU.max).then_inc(s_cst, 1)
                norm1(0, 0)
                dve.wait_ge(s_tanh0, 1)
                sn, ta = scratch[:, 5, 0:64], scratch[:, 5, 64:128]
                link(dve.scalar_tensor_tensor(out=ta, in0=ta, scalar=1.0, in1=sn, op0=ALU.add, op1=ALU.mult))
                dve.tensor_scalar(scratch[:, 4, 64:128], ta, 0.5, None, ALU.mult).then_inc(s_emb, 1)
                apply1(0)
                dve.wait_ge(s_id, 3)
                link(dve.tensor_copy(ident_b[:], ident[:]))
                dve.tensor_copy(ident_r[:], ident[:]).then_inc(s_split, 1)
                ring = PT[:].rearrange("p a t s -> p (a t s)")

                def split_weight(k, hl, raw):
                    dve.wait_ge(ld_w[k], 16)
                    link(dve.tensor_copy(hl[:, 0], raw))
                    return dve.tensor_tensor(hl[:, 1], raw, hl[:, 0].bitcast(F32), ALU.subtract)

                raws = [ring[:, k * NC * D:(k + 1) * NC * D].rearrange("p (k n) -> p k n", k=NC) for k in range(4)]
                split_weight(0, wq_hl, raws[0])
                split_weight(1, wk_hl, raws[1]).then_inc(s_split, 1)
                dve.wait_ge(ld_c, 16 * 11)
                link(dve.tensor_copy(sel[:].rearrange("h c p -> h (c p)"), scratch[0:2 * H, 7]))
                link(dve.tensor_scalar(bqk[:, :, 0], bqk[:, :, 0], HD ** -0.5, None, ALU.mult))
                link(dve.tensor_scalar(b1s[:], b1c[:], GELU / 2, None, ALU.mult))
                dve.wait_ge(s_embmm, 1)
                for m in range(4):
                    link(dve.tensor_scalar(emb[:, m, :], M2[:, 0, m * B:(m + 1) * B], bad[:, m:m + 1],
                                           1.0 if m < 2 else 0.0, ALU.add, ALU.add))
                cur_copy(0, 0)
                x_split(0, 0)
                split_weight(2, wv_hl, raws[2]).then_inc(s_split, 1)
                qk_split(0, 0)
                split_weight(3, wo_hl, raws[3]).then_inc(s_split, 1)
                split_weight(4, w1_hl, ring[:, 2048:4096].rearrange("p (k n) -> p k n", k=NC)).then_inc(s_split, 1)
                qk_split(0, 1)

            def edge_coefficients(end):
                sg = 1.0 if end == 0 else -1.0
                for k, (cb, ca, c2_) in enumerate(((1.0, 1.5, -3.0), (-2.5, -2.0, 4.0), (2.0, 0.5, -1.0), (-0.5, 0.0, 0.0))):
                    o, k = (k, k) if end == 0 else (S - 1 - k, 3 - k)
                    link(dve.tensor_scalar(edge[:, :, end, k:k + 1], gR[:, :, o:o + 1], sg * ca, None, ALU.mult))
                    link(dve.scalar_tensor_tensor(out=edge[:, :, end, k:k + 1], in0=gC[:, :, o:o + 1], scalar=cb,
                                                  in1=edge[:, :, end, k:k + 1], op0=ALU.mult, op1=ALU.add))
                    link(dve.tensor_scalar(edge[:, :, 2 + end, k:k + 1], gB2[:, :, o:o + 1], sg * c2_, None, ALU.mult))

            def grid_coefficients():
                link(dve.tensor_scalar(gA0, gA0, -2.0, None, ALU.mult))
                link(dve.tensor_tensor(gL, gC, gR, ALU.add))
                link(dve.tensor_tensor(gR, gC, gR, ALU.subtract))
                link(dve.tensor_scalar(gL, gL, 0.5, None, ALU.mult))
                link(dve.tensor_scalar(gR, gR, 0.5, None, ALU.mult))
                link(dve.tensor_scalar(gC, gC, -1.0, None, ALU.mult))

            def split_w2(q):
                hi, lo = (w2_hl[:, a, 2 * q:2 * q + 2] for a in (0, 1))
                link(dve.tensor_copy(hi, w2_raw[q][:]))
                dve.tensor_tensor(lo, w2_raw[q][:], hi.bitcast(F32), ALU.subtract).then_inc(s_w2, 1)

            def rest_of_setup(h):
                if h == 17:
                    dve.wait_ge(ld_w2, 16 * len(w2_raw))
                if h in (17, 19, 21, 23):
                    split_w2((h - 17) // 2)
                if h == 24:
                    dve.wait_ge(ld_g, 16 * 7)
                if h in (24, 25):
                    link(dve.tensor_copy(sten_w[:, h - 24], sten_raw[h - 24][:]))
                if h in (26, 27):
                    edge_coefficients(h - 26)
                if h == 28:
                    grid_coefficients()

            def body(j, par, att, nxt, post, sten):
                i = j * 2 + par
                b = i - 1
                d = i - 2
                zero = isinstance(i, int) and i == 0
                first = isinstance(b, int) and b == 0
                dfirst = isinstance(d, int) and d == 0
                for h in range(2 * H):
                    n = h // 2
                    if h % 2 == 0 and att:
                        by_itself(dve, (s_S, i * H + n + 1), *([(ld_bias[n // GROUP], i * 32 + 32)] if n % GROUP == 0 else []))
                        for t in range(NT):
                            dve.tensor_tensor_reduce(out=bias[:, n // GROUP % 2, n % GROUP, t], in0=pS[n % 2][:, t],
                                                     in1=bias[:, n // GROUP % 2, n % GROUP, t], scale=-1.0, scalar=HUGE,
                                                     op0=ALU.add, op1=ALU.min,
                                                     accum_out=nmax[:, n, t:t + 1]).then_inc(s_ttr, 1)
                    if h % 2 == 1 and (n - 2) % H not in PT_ON_ACT:
                        if n >= 2 and att:
                            probs_evac(i, n - 2)
                        if n < 2 and post:
                            probs_evac(b, n - 2 + H)
                    if zero:
                        rest_of_setup(h)
                    if nxt and h == AT_DVE["norm1"]:
                        cur_copy(i + 1, 1 - par)
                        norm1(i + 1, 1 - par)
                    if nxt and h == AT_DVE["x"]:
                        apply1(i + 1)
                    if nxt and h == AT_DVE["x split"]:
                        if post:
                            dve.wait_ge(s_wo, i)
                        x_split(i + 1, 1 - par)
                    for c in range(NC):
                        if nxt and h == AT_DVE["qk split"][c]:
                            qk_split(i + 1, c)
                    if att and h == AT_DVE["v"]:
                        dve.wait_ge(s_v, i + 1)
                        if zero:
                            dve.wait_ge(s_zero, 3)
                        if not zero:
                            dve.wait_ge(s_ctx, i * NG)
                        for t in range(NT):
                            for e in range(2):
                                last = dve.tensor_tensor(
                                    V[:, t, e::2, HD * e:HD * e + HD],
                                    M0[:, t, :].rearrange("p (h e d) -> p h e d", e=2, d=HD)[:, :, e, :],
                                    bv_row[:].rearrange("p (h e d) -> p h e d", e=2, d=HD)[:, :, e, :], ALU.add)
                        last.then_inc(s_vev, 1)
                    if post and h == AT_DVE["rec"]:
                        dve.wait_ge(s_exp, i * 32)
                        if not first:
                            dve.wait_ge(s_recT, b)
                        dve.reciprocal(recf[:], sums[:, 1 - par]).then_inc(s_recf, 1)
                        dve.wait_ge(s_recf, i)
                        dve.tensor_copy(rec[:, :, 0], recf[:]).then_inc(s_rhi, 1)
                        dve.wait_ge(s_rhi, i)
                        dve.tensor_tensor(rec[:, :, 1], recf[:], rec[:, :, 0].bitcast(F32), ALU.subtract).then_inc(s_rec, 1)
                    if post and h == AT_DVE["context"]:
                        dve.wait_ge(s_ctx, i * NG)
                        dve.wait_ge(s_rTs, i)
                        if not first:
                            dve.wait_ge(s_x2b, b * 2)
                        dve.tensor_tensor(cn[:], pC_[:], rTs[:], ALU.mult).then_inc(s_cn, 1)
                        dve.wait_ge(s_cn, i)
                        dve.tensor_copy(cT[:, 0], cn[:]).then_inc(s_chi, 1)
                        dve.wait_ge(s_chi, i)
                        dve.tensor_tensor(cT[:, 1], cn[:], cT[:, 0].bitcast(F32), ALU.subtract).then_inc(s_chl, 1)
                    if post and h == AT_DVE["x2"]:
                        dve.wait_ge(s_wo, i)
                        for t in range(NT):
                            dve.tensor_tensor(x2[:, t], M0[:, t], bo_row[:], ALU.add).then_inc(s_x2, 1)
                        dve.wait_ge(s_x2, i * 2)
                        norm(b, x2, stat2, mv2, s_stat2, s_mv2)
                    if post and h == AT_DVE["h"]:
                        dve.wait_ge(s_rs2, i)
                        if nxt:
                            dve.wait_ge(s_xT, i + 2)
                        apply_norm(hn, x2, mv2, rs2, s_hn)
                    if post and h == AT_DVE["h split"]:
                        dve.wait_ge(s_hTf, i * 2)
                        if sten:
                            dve.wait_ge(s_st, d + 1)
                        dve.tensor_copy(hT[:, 0], hTf[:]).then_inc(s_hhi, 1)
                        dve.wait_ge(s_hhi, i)
                        dve.tensor_tensor(hT[:, 1], hTf[:], hT[:, 0].bitcast(F32), ALU.subtract).then_inc(s_hhl, 1)
                    for f in range(NF // 2):
                        if post and h == AT_DVE["gelu"][f]:
                            dve.wait_ge(s_th1, b * 4 + f + 1)
                            for m in range(2):
                                last = dve.scalar_tensor_tensor(out=th[:, f % 2, m], in0=(M0, M1)[f % 2][:, m],
                                                                scalar=b1c[:, 2 * f + m:2 * f + m + 1], in1=th[:, f % 2, m],
                                                                op0=ALU.add, op1=ALU.mult)
                            last.then_inc(s_gf, 1)
                        if post and h == AT_DVE["gelu high"][f]:
                            dve.wait_ge(s_gf, b * 4 + f + 1)
                            if f == 0 and not first:
                                dve.wait_ge(s_f2, b)
                            dve.tensor_copy(g_hl[:, 0, 2 * f:2 * f + 2], th[:, f % 2]).then_inc(s_ghi, 1)
                    m = now(AT_DVE["x3"], h, post, sten, i)
                    if m is not None:
                        dve.wait_ge(s_f2, m + 1)
                        dve.wait_ge(s_x2b, (m + 1) * 2)
                        if not (isinstance(m, int) and m == 0):
                            dve.wait_ge(s_zf, m)
                        dve.tensor_copy(dcur[:], dt_row[:, column(m)]).then_inc(s_dcur, 1)
                        dve.scalar_tensor_tensor(out=x3[:], in0=M2[:], scalar=0.5, in1=x2b[:],
                                                 op0=ALU.mult, op1=ALU.add).then_inc(s_x3, 1)
                    if sten and h == AT_DVE["edges"]:
                        dve.wait_ge(s_x3, d + 1)
                        for end in range(2):
                            f4 = x3[:, :, 0:4] if end == 0 else x3[:, :, S - 4:S]
                            for kind in range(2):
                                dve.tensor_tensor(ed[:, :, 2 * kind + end, :], f4, edge[:, :, 2 * kind + end, :], ALU.mult)\
                                    .then_inc(s_ed, 1)
                    if sten and h == AT_DVE["edge sums"]:
                        dve.wait_ge(s_ed, (d + 1) * 4)
                        dve.tensor_reduce(out=tt[:, :, 0:S:S - 1], in_=ed[:, :, 0:2, :], axis=AXES.X, op=ALU.add).then_inc(s_te, 1)
                        dve.tensor_reduce(out=u1e[:], in_=ed[:, :, 2:4, :], axis=AXES.X, op=ALU.add).then_inc(s_e1, 1)
                        dve.wait_ge(s_e1, d + 1)
                        dve.wait_ge(s_a0f, d + 1)
                        dve.tensor_tensor(u1[:, :, 0:S:S - 1], u1[:, :, 0:S:S - 1], u1e[:], ALU.add).then_inc(s_u1e, 1)
                    if sten and h == AT_DVE["u high"]:
                        dve.wait_ge(s_u1, d + 1)
                        dve.wait_ge(s_u1e, d + 1)
                        dve.wait_ge(s_u2, d + 1)
                        dve.tensor_copy(u1_hl[:, 0], u1[:]).then_inc(s_uhi, 1)
                        dve.tensor_copy(u2_hl[:, 0], u2[:]).then_inc(s_uhi, 1)
                    if sten and h == AT_DVE["z"]:
                        dve.wait_ge(s_st, d + 1)
                        dve.wait_ge(s_tt, (d + 1) * 2)
                        dve.wait_ge(s_te, d + 1)
                        dve.tensor_tensor(yy[:], M2[:], tt[:], ALU.add).then_inc(s_y, 1)
                        dve.wait_ge(s_y, d + 1)
                        dve.wait_ge(s_dcur, d + 1)
                        dve.scalar_tensor_tensor(out=zf[:], in0=yy[:], scalar=dcur[:, 0:1], in1=x3[:],
                                                 op0=ALU.mult, op1=ALU.add).then_inc(s_zf, 1)

            run(dve, prologue, body)


def _stencil_matrices(np):
    m = np.zeros((2, S, S), np.float32)
    for k in range(1, S - 1):
        m[0, k + 1, k], m[0, k - 1, k] = 0.25, -0.25
        m[1, k + 1, k], m[1, k, k], m[1, k - 1, k] = 0.5, -1.0, 0.5
    m[0, 0:3, 0] = (-0.75, 1.0, -0.25)
    m[0, S - 3:, S - 1] = (0.25, -1.0, 0.75)
    m[1, 0:4, 0] = (1.0, -2.5, 2.0, -0.5)
    m[1, S - 4:, S - 1] = (-0.5, 2.0, -2.5, 1.0)
    return m


def kernel(**inputs):
    import numpy as np
    import concourse.bacc as bacc
    from concourse.bass_utils import run_bass_kernel_spmd

    def stacked(w):
        w = np.asarray(w)
        return w.reshape(-1, NC, 4, 2, HD).transpose(0, 1, 3, 4, 2).reshape(w.shape)

    given = {k: np.asarray(v) for k, v in inputs.items()}
    layer = lambda name: given["L0_cond_" + name]
    arrays = {
        "x": given["x"], "itok": given["itok_B_34_63"], "fside": given["fside_Bx16xSxS_0"], "dt": given["condB_dt"],
        "mask": given["mask_Bx1xSxS_bk0"].view(np.int32).reshape(B, S, S // 4),
        "W_ada": layer("W_ada"), "b_ada": layer("b_ada"),
        "Wq": stacked(layer("Wq")), "bq": stacked(layer("bq")), "Wk": stacked(layer("Wk")), "bk": stacked(layer("bk")),
        "Wv": layer("Wv"), "bv": layer("bv"), "Wo": layer("Wo"), "bo": layer("bo"),
        "W1": layer("W1"), "b1": layer("b1"), "W2": layer("W2"), "b2": layer("b2"),
        "g2": layer("g2"), "beta2": layer("beta2"),
        "A_grid": given["L1_cond_A_grid"], "B_grid": given["L1_cond_B_grid"],
        "freqs": np.exp(np.arange(P, dtype=np.float32) * np.float32(-np.log(10000.0) / (P - 1))),
        "stencils": _stencil_matrices(np),
        "selector": np.tile(np.repeat(np.eye(H, dtype=np.float32), HD, axis=1), (2, 1)).reshape(2 * H, NC, P),
    }
    nc = bacc.Bacc("TRN2", target_bir_lowering=False, num_devices=1)
    args = []
    for name, a in arrays.items():
        arrays[name] = a = np.ascontiguousarray(a)
        args.append(nc.dram_tensor(name, a.shape, mybir.dt.from_np(a.dtype), kind="ExternalInput").ap())
    out = nc.dram_tensor("out", (B, S, D), F32, kind="ExternalOutput").ap()
    order = ["x", "itok", "fside", "dt", "mask", "W_ada", "b_ada", "Wq", "bq", "Wk", "bk", "Wv", "bv", "Wo", "bo",
             "W1", "b1", "W2", "b2", "g2", "beta2", "A_grid", "B_grid", "freqs", "stencils", "selector"]
    named = dict(zip(arrays, args))
    build(nc, *[named[n] for n in order], out)
    result = run_bass_kernel_spmd(nc, [arrays], core_ids=[0])
    return result.results[0]["out"]
```
